# Optimizing a Trainium2 kernel written in Bass

```python
import numpy as np
import jax
import jax.numpy as jnp

def _softmax(x, axis=-1):
    return jax.nn.softmax(x, axis=axis)

def _gelu(x):
    return jax.nn.gelu(x, approximate=True)

def _silu(x):
    return jax.nn.silu(x)

def _sigmoid(x):
    return jax.nn.sigmoid(x)

def _layernorm(x, axis=-1, eps=1e-05):
    m = jnp.mean(x, axis=axis, keepdims=True)
    v = jnp.var(x, axis=axis, keepdims=True)
    return (x - m) / jnp.sqrt(v + eps)

def _scatter_add(tgt, idx, src, axis=0):
    return tgt.at[idx].add(src)

def _segment_sum(src, seg, n):
    return jax.ops.segment_sum(src, seg, n)
kernel_name = 'mk_cond_resid_d4_seqx_r8_c7121c'

def setup_inputs(seed: int=0):
    np.random.seed(seed)
    _w = jnp.asarray

    def _rec_inputs():
        import jax
        import jax.numpy as jnp
        _rk = jax.random.key(seed)
        x = 7.22e-05 + 1 * jax.random.normal(jax.random.fold_in(_rk, 1), (16, 128, 256), jnp.float32)
        _lenS = 128 - jax.random.randint(jax.random.fold_in(_rk, 7), (16,), 0, max(1, 128 // 4) + 1, jnp.int32)
        _lenS2 = 128 - jax.random.randint(jax.random.fold_in(_rk, 8), (16,), 0, max(1, 128 // 4) + 1, jnp.int32)
        cond_2048 = jax.random.bernoulli(jax.random.fold_in(_rk, 11), 0.8975, (16, 256)).astype(jnp.float32)
        return (x, cond_2048)
    x, cond_2048 = _rec_inputs()

    def _L0_cond_setup():
        import jax, jax.numpy as jnp
        import numpy as np
        import math
        D_MODEL = 128
        NUM_HEAD = 16
        NEG_INF = -1e+30
        key = jax.random.key(seed)
        k_x, k_m, k_q, k_k, k_v = jax.random.split(key, 5)
        B, C, T = (4, D_MODEL, 256)
        x = jax.random.normal(k_x, (B, C, T), dtype=jnp.float32)
        mask = (jax.random.uniform(k_m, (B, T)) < 0.9).astype(jnp.float32)
        limit = math.sqrt(6.0 / (C + C))
        Wq = jax.random.uniform(k_q, (C, C), minval=-limit, maxval=limit, dtype=jnp.float32)
        Wk = jax.random.uniform(k_k, (C, C), minval=-limit, maxval=limit, dtype=jnp.float32)
        Wv = jax.random.uniform(k_v, (C, C), minval=-limit, maxval=limit, dtype=jnp.float32)
        b = jnp.zeros((1,), dtype=jnp.float32)
        return {'x': x, 'mask': mask, 'Wq': Wq, 'Wk': Wk, 'Wv': Wv, 'b': b}
    _L0_cond_all = _L0_cond_setup()
    _L0_cond_in = {k: v for k, v in _L0_cond_all.items() if k in ('Wq', 'Wk', 'Wv', 'b')}
    del _L0_cond_all

    def _L1_cond_setup():
        import jax, jax.numpy as jnp
        import numpy as np
        HEADS = 16
        EPS = 1e-06

        def _rms_norm(x, g):
            xf = x.astype(jnp.float32)
            y = xf * jax.lax.rsqrt(jnp.mean(xf * xf, axis=-1, keepdims=True) + EPS)
            return y.astype(x.dtype) * g
        key = jax.random.key(seed)
        ks = jax.random.split(key, 6)
        b, n, dim, emb_dim = (4, 256, 256, 256)
        d_head = dim // HEADS
        return {'x': jax.random.normal(ks[0], (b, n, dim), jnp.float32), 'emb': jax.random.normal(ks[1], (b, 1, emb_dim), jnp.float32), 'W_emb': jax.random.normal(ks[2], (emb_dim, 2 * dim), jnp.float32) * emb_dim ** (-0.5), 'b_emb': jnp.zeros((2 * dim,), jnp.float32), 'g_norm': jnp.ones((dim,), jnp.float32), 'W_qkv': jax.random.normal(ks[3], (dim, 3 * dim), jnp.float32) * dim ** (-0.5), 'g_q': jnp.ones((d_head,), jnp.float32), 'g_k': jnp.ones((d_head,), jnp.float32), 'W_out': jax.random.normal(ks[4], (dim, dim), jnp.float32) * dim ** (-0.5)}
    _L1_cond_all = _L1_cond_setup()
    _L1_cond_in = {k: v for k, v in _L1_cond_all.items() if k in ('W_emb', 'b_emb', 'g_norm', 'W_qkv', 'g_q', 'g_k', 'W_out')}
    del _L1_cond_all

    def _L2_cond_setup():
        import jax, jax.numpy as jnp
        import numpy as np
        DIM = 256
        H = 16
        DH = 128
        INNER = H * DH
        MLP = 4 * DIM
        B, T = (2, 256)
        EPS = 1e-06

        def _ln(x):
            mu = jnp.mean(x, axis=-1, keepdims=True)
            var = jnp.var(x, axis=-1, keepdims=True)
            return (x - mu) * jax.lax.rsqrt(var + EPS)
        key = jax.random.key(seed)
        ks = jax.random.split(key, 12)
        s = 0.02
        return {'x': jax.random.normal(ks[0], (B, T, DIM), jnp.float32), 'timestep_embed': jax.random.normal(ks[1], (B, DIM), jnp.float32), 'ada_w': jax.random.normal(ks[2], (DIM, 6 * DIM), jnp.float32) * s, 'ada_b': jnp.zeros((6 * DIM,), jnp.float32), 'qkv_w': jax.random.normal(ks[3], (DIM, 3 * INNER), jnp.float32) * s, 'qkv_b': jnp.zeros((3 * INNER,), jnp.float32), 'out_w': jax.random.normal(ks[4], (INNER, DIM), jnp.float32) * s, 'out_b': jnp.zeros((DIM,), jnp.float32), 'ffn_w1': jax.random.normal(ks[5], (DIM, MLP), jnp.float32) * s, 'ffn_b1': jnp.zeros((MLP,), jnp.float32), 'ffn_w2': jax.random.normal(ks[6], (MLP, DIM), jnp.float32) * s, 'ffn_b2': jnp.zeros((DIM,), jnp.float32)}
    _L2_cond_all = _L2_cond_setup()
    _L2_cond_in = {k: v for k, v in _L2_cond_all.items() if k in ('ada_w', 'ada_b', 'qkv_w', 'qkv_b', 'out_w', 'out_b', 'ffn_w1', 'ffn_b1', 'ffn_w2', 'ffn_b2')}
    del _L2_cond_all

    def _L3_cond_setup():
        import jax, jax.numpy as jnp
        import numpy as np
        B, T, D = (16, 128, 256)
        key = jax.random.key(seed)
        k0, k1, k2, k3 = jax.random.split(key, 4)
        scale = 1.0 / np.sqrt(D)
        return {'initial_state': jax.random.normal(k0, (B, D), jnp.float32), 'inputs': jax.random.normal(k1, (B, T, D), jnp.float32), 'W_ih': jax.random.normal(k2, (D, 3 * D), jnp.float32) * scale, 'W_hh': jax.random.normal(k3, (D, 3 * D), jnp.float32) * scale, 'b_ih': jnp.zeros((3 * D,), jnp.float32), 'b_hh': jnp.zeros((3 * D,), jnp.float32)}
    _L3_cond_all = _L3_cond_setup()
    _L3_cond_in = {k: v for k, v in _L3_cond_all.items() if k in ('W_ih', 'W_hh', 'b_ih', 'b_hh')}
    del _L3_cond_all
    return {'x': x, 'cond_2048': cond_2048, 'L0_cond_Wq': _L0_cond_in['Wq'], 'L0_cond_Wk': _L0_cond_in['Wk'], 'L0_cond_Wv': _L0_cond_in['Wv'], 'L0_cond_b': _L0_cond_in['b'], 'L1_cond_W_emb': _L1_cond_in['W_emb'], 'L1_cond_b_emb': _L1_cond_in['b_emb'], 'L1_cond_g_norm': _L1_cond_in['g_norm'], 'L1_cond_W_qkv': _L1_cond_in['W_qkv'], 'L1_cond_g_q': _L1_cond_in['g_q'], 'L1_cond_g_k': _L1_cond_in['g_k'], 'L1_cond_W_out': _L1_cond_in['W_out'], 'L2_cond_ada_w': _L2_cond_in['ada_w'], 'L2_cond_ada_b': _L2_cond_in['ada_b'], 'L2_cond_qkv_w': _L2_cond_in['qkv_w'], 'L2_cond_qkv_b': _L2_cond_in['qkv_b'], 'L2_cond_out_w': _L2_cond_in['out_w'], 'L2_cond_out_b': _L2_cond_in['out_b'], 'L2_cond_ffn_w1': _L2_cond_in['ffn_w1'], 'L2_cond_ffn_b1': _L2_cond_in['ffn_b1'], 'L2_cond_ffn_w2': _L2_cond_in['ffn_w2'], 'L2_cond_ffn_b2': _L2_cond_in['ffn_b2'], 'L3_cond_W_ih': _L3_cond_in['W_ih'], 'L3_cond_W_hh': _L3_cond_in['W_hh'], 'L3_cond_b_ih': _L3_cond_in['b_ih'], 'L3_cond_b_hh': _L3_cond_in['b_hh']}

def reference(x, cond_2048, L0_cond_Wq, L0_cond_Wk, L0_cond_Wv, L0_cond_b, L1_cond_W_emb, L1_cond_b_emb, L1_cond_g_norm, L1_cond_W_qkv, L1_cond_g_q, L1_cond_g_k, L1_cond_W_out, L2_cond_ada_w, L2_cond_ada_b, L2_cond_qkv_w, L2_cond_qkv_b, L2_cond_out_w, L2_cond_out_b, L2_cond_ffn_w1, L2_cond_ffn_b1, L2_cond_ffn_w2, L2_cond_ffn_b2, L3_cond_W_ih, L3_cond_W_hh, L3_cond_b_ih, L3_cond_b_hh):
    import jax
    import jax.numpy as jnp

    def _L0_cond_ref(x, mask, Wq, Wk, Wv, b):
        import jax, jax.numpy as jnp
        import numpy as np
        import math
        D_MODEL = 128
        NUM_HEAD = 16
        NEG_INF = -1e+30
        B, C, T = x.shape
        H = NUM_HEAD
        Dh = C // H

        def proj(W):
            y = jnp.einsum('oc,bct->bto', W, x)
            return y.reshape(B, T, H, Dh).transpose(0, 2, 1, 3)
        Q, K, V = (proj(Wq), proj(Wk), proj(Wv))
        att = jnp.einsum('bhqd,bhkd->bhqk', Q, K) * (1.0 / math.sqrt(Dh))
        att = att + b[0]
        m = mask[:, None, None, :]
        att = att * m + (1.0 - m) * NEG_INF
        att = jax.nn.softmax(att, axis=-1)
        y = jnp.einsum('bhqk,bhkd->bhqd', att, V)
        y = y.transpose(0, 2, 1, 3).reshape(B, T, C)
        return y.transpose(0, 2, 1)

    def _L1_cond_ref(x, emb, W_emb, b_emb, g_norm, W_qkv, g_q, g_k, W_out):
        import jax, jax.numpy as jnp
        import numpy as np
        HEADS = 16
        EPS = 1e-06

        def _rms_norm(x, g):
            xf = x.astype(jnp.float32)
            y = xf * jax.lax.rsqrt(jnp.mean(xf * xf, axis=-1, keepdims=True) + EPS)
            return y.astype(x.dtype) * g
        b, n, dim = x.shape
        h = HEADS
        d = dim // h
        scale_shift = emb @ W_emb + b_emb
        scale, shift = jnp.split(scale_shift, 2, axis=-1)
        xn = _rms_norm(x, g_norm) * (1.0 + scale) + shift
        qkv = xn @ W_qkv
        qkv = qkv.reshape(b, n, 3, h, d)
        q, k, v = jnp.moveaxis(qkv, 2, 0)
        q = jnp.swapaxes(q, 1, 2)
        k = jnp.swapaxes(k, 1, 2)
        v = jnp.swapaxes(v, 1, 2)
        q = _rms_norm(q, g_q)
        k = _rms_norm(k, g_k)
        logits = jnp.einsum('bhqd,bhkd->bhqk', q, k) * d ** (-0.5)
        attn = jax.nn.softmax(logits, axis=-1)
        o = jnp.einsum('bhqk,bhkd->bhqd', attn, v)
        o = jnp.swapaxes(o, 1, 2).reshape(b, n, dim)
        return o + o @ W_out

    def _L2_cond_ref(x, timestep_embed, ada_w, ada_b, qkv_w, qkv_b, out_w, out_b, ffn_w1, ffn_b1, ffn_w2, ffn_b2):
        import jax, jax.numpy as jnp
        import numpy as np
        DIM = 256
        H = 16
        DH = 128
        INNER = H * DH
        MLP = 4 * DIM
        B, T = (2, 256)
        EPS = 1e-06

        def _ln(x):
            mu = jnp.mean(x, axis=-1, keepdims=True)
            var = jnp.var(x, axis=-1, keepdims=True)
            return (x - mu) * jax.lax.rsqrt(var + EPS)
        Bc, Tc, D = x.shape
        ada = (timestep_embed @ ada_w + ada_b)[:, None, :]
        shift1, scale1, gate1, shift2, scale2, gate2 = jnp.split(ada, 6, axis=-1)
        x1 = _ln(x) * (1.0 + scale1) + shift1
        qkv = (x1 @ qkv_w + qkv_b).reshape(Bc, Tc, 3, H, DH)
        q, k, v = (qkv[:, :, 0], qkv[:, :, 1], qkv[:, :, 2])
        scale = DH ** (-0.5)
        attn = jnp.einsum('bthd,bshd->bhts', q, k) * scale
        attn = jax.nn.softmax(attn, axis=-1)
        attn_out = jnp.einsum('bhts,bshd->bthd', attn, v).reshape(Bc, Tc, INNER)
        attn_out = attn_out @ out_w + out_b
        x = x + gate1 * attn_out
        x2 = _ln(x) * (1.0 + scale2) + shift2
        h = jax.nn.gelu(x2 @ ffn_w1 + ffn_b1, approximate=False)
        x = x + gate2 * (h @ ffn_w2 + ffn_b2)
        return x

    def _L3_cond_ref(initial_state, inputs, W_ih, W_hh, b_ih, b_hh):
        import jax, jax.numpy as jnp
        import numpy as np
        B, T, D = (16, 128, 256)
        "ScanOverTime(GRU cell): sequential per-timestep module call with\n            dict-state passing; merge_dict_trees stacks the per-step\n            'state_predicted' tensors along axis=1 -> [B, T, D]."

        def cell(h, x):
            gi = x @ W_ih + b_ih
            gh = h @ W_hh + b_hh
            i_r, i_z, i_n = jnp.split(gi, 3, axis=-1)
            h_r, h_z, h_n = jnp.split(gh, 3, axis=-1)
            r = jax.nn.sigmoid(i_r + h_r)
            z = jax.nn.sigmoid(i_z + h_z)
            n = jnp.tanh(i_n + r * h_n)
            h_new = (1.0 - z) * n + z * h
            return (h_new, h_new)
        xs = jnp.swapaxes(inputs, 0, 1)
        _, hs = jax.lax.scan(cell, initial_state, xs)
        return jnp.swapaxes(hs, 0, 1)
    x = x + _L0_cond_ref(x, cond_2048, L0_cond_Wq, L0_cond_Wk, L0_cond_Wv, L0_cond_b)
    x = x + _L1_cond_ref(x, cond_2048[:, None, :], L1_cond_W_emb, L1_cond_b_emb, L1_cond_g_norm, L1_cond_W_qkv, L1_cond_g_q, L1_cond_g_k, L1_cond_W_out)
    x = x + _L2_cond_ref(x, cond_2048, L2_cond_ada_w, L2_cond_ada_b, L2_cond_qkv_w, L2_cond_qkv_b, L2_cond_out_w, L2_cond_out_b, L2_cond_ffn_w1, L2_cond_ffn_b1, L2_cond_ffn_w2, L2_cond_ffn_b2)
    x = x + _L3_cond_ref(cond_2048, x, L3_cond_W_ih, L3_cond_W_hh, L3_cond_b_ih, L3_cond_b_hh)
    return x

_drawn_inputs = setup_inputs


def setup_inputs(seed=0):
    import zlib

    import numpy as np

    out = dict(_drawn_inputs(seed))
    spreads = {'L1_cond_b_emb': (0.0, 0.1),
     'L1_cond_g_norm': (1.0, 0.2),
     'L1_cond_g_q': (1.0, 0.539),
     'L1_cond_g_k': (1.0, 0.6),
     'L2_cond_ada_b': (0.0, 0.726),
     'L2_cond_qkv_b': (0.0, 0.8),
     'L2_cond_out_b': (0.0, 0.8),
     'L2_cond_ffn_b1': (0.0, 0.8),
     'L2_cond_ffn_b2': (0.0, 0.8),
     'L3_cond_b_ih': (0.0, 0.793),
     'L3_cond_b_hh': (0.0, 2.0)}
    factors = {'L2_cond_ffn_w1': 4.866, 'L2_cond_ffn_w2': 4.614}
    for name, (base, spread) in spreads.items():
        noise = np.random.default_rng([zlib.crc32(name.encode()), seed]).standard_normal(out[name].shape)
        drawn = base * np.exp(spread * noise) if base else spread * noise
        out[name] = jnp.asarray(drawn.astype(out[name].dtype))
    for name, factor in factors.items():
        out[name] = (out[name] * factor).astype(out[name].dtype)
    return out
```

```python
from contextlib import ExitStack

import concourse.bass as bass
from concourse import mybir

ALU = mybir.AluOpType
ACT = mybir.ActivationFunctionType
AX = mybir.AxisListType
F32 = mybir.dt.float32
BF16 = mybir.dt.bfloat16

P = 128
B, N, D = 16, 128, 256
KT = D // P
H = 16
NEG = -1e30
NPART = 3

DH0 = N // H
TERMS = NPART * NPART * DH0
ROWS0 = TERMS + NPART
PAIRS = H // 2
ORDER0 = [4 * (n % 4) + n // 4 for n in range(H)]
VBLK = 160

DH1 = D // H
G1 = 4
EPS = 1e-6

DH2 = 128
INNER = H * DH2
MLP = 4 * D
SCALE2 = float(DH2) ** -0.5
G2 = H // 4

GATES = 3 * KT
UNROLL = 8


def carry(eng, m):
    eng.sem_inc(m.passed, 1)


class Chain:

    def __init__(self, eng, sem, base=0):
        self.eng, self.sem, self.base, self.n = eng, sem, base, 0

    def link(self, ins):
        self.n += 1
        ins.then_inc(self.sem, 1)
        self.eng.wait_ge(self.sem, self.base + self.n)


def program(nc, a, out):
    with ExitStack() as ctx:
        def sb(name, shape, dt=F32):
            return ctx.enter_context(nc.sbuf_tensor(name, shape, dt))

        def sem(name):
            return ctx.enter_context(nc.semaphore(name))

        m = Mem()
        m.ps = ctx.enter_context(nc.psum_tensor("ps", [P, 8, 512], F32))
        m.X = sb("X", [P, B, D])
        m.ident = sb("ident", [P, P])
        m.identb = sb("identb", [P, P], BF16)
        m.condT = sb("condT", [P, KT, B])
        m.mod1 = sb("mod1", [P, 2 * KT, B])
        m.ada = sb("ada", [P, 6 * KT, B])
        m.A1 = sb("A1", [P, KT, B])
        m.gb = sb("gb", [P, 2 * KT, B])
        m.nhalf = sb("nhalf", [P, 2 * H])
        m.w_qkv1 = sb("w_qkv1", [P, KT, 3 * D])
        m.w_out1 = sb("w_out1", [P, KT, D])
        m.w_ih = sb("w_ih", [P, KT, 3 * D])
        m.whp = sb("whp", [P, NPART, KT, 3 * D], BF16)
        m.big = sb("big", [P, KT * 3 * INNER])
        m.ring = sb("ring", [P, 8192])
        m.work = sb("work", [P, 13824])
        m.XA = m.work[:, 9728:13824].rearrange("p (b d) -> p b d", b=B)
        m.cols = sb("cols", [P, 512])
        m.ssq = m.cols[:, 480:480 + B]
        m.passed = sem("passed")
        m.dma_x = sem("x_loaded")
        m.dma_w = [sem(f"w_loaded{k}") for k in range(4)]
        setup(nc, a, m, sem)
        phase_l0(nc, a, m, sem)
        phase_l1(nc, a, m, sem)
        phase_l2(nc, a, m, sem)
        phase_ffn(nc, a, m, sem)
        phase_gru(nc, a, m, sem, out)


class Mem:
    pass


def setup(nc, a, m, sem):
    cols = m.cols
    bcol = cols[:, 0:16].rearrange("p (c o) -> p c o", o=1)
    loaded, made, mod_ps, mod_sb = sem("setup_loaded"), sem("setup_made"), sem("mod_ps"), sem("mod_sb")
    vstep, gstep, split = sem("setup_vstep"), sem("setup_gstep"), sem("whh_split")
    m.split = split
    w_emb = m.work[:, 0:1024].rearrange("p (k n) -> p k n", k=KT)
    ada_w = m.work[:, 1024:4096].rearrange("p (k n) -> p k n", k=KT)
    w_hh = m.work[:, 4096:5632]
    rest = m.work[:, 5632:7168]
    whp = m.whp[:].rearrange("p a k n -> p a (k n)")
    b_emb = cols[:, 0:4]
    ada_b = cols[:, 4:16]
    g_norm = cols[:, 16:18]
    out_b = cols[:, 18:20]
    ffn_b2 = cols[:, 20:22]
    tmp = cols[:, 32:64].rearrange("p (k b) -> p k b", k=KT)
    bc = lambda v: v.unsqueeze(2).broadcast_to([P, v.shape[1], B])
    with nc.Block() as block:
        @block.sync
        def _(sp):
            for k, v in ((a["L1_cond_W_emb"], w_emb), (a["L2_cond_ada_w"], ada_w)):
                sp.dma_start(v, k.rearrange("(k p) n -> p k n", p=P)).then_inc(loaded, 16)
            sp.dma_start(m.condT[:], a["condT"].rearrange("(k p) b -> p k b", p=P)).then_inc(loaded, 16)
            for src, dst in (("L1_cond_b_emb", b_emb), ("L2_cond_ada_b", ada_b), ("L1_cond_g_norm", g_norm),
                             ("L2_cond_out_b", out_b), ("L2_cond_ffn_b2", ffn_b2)):
                sp.dma_start(dst, a["col_" + src]).then_inc(loaded, 16)
            sp.dma_start(w_hh.rearrange("p (k n) -> p k n", k=KT),
                         a["L3_cond_W_hh"].rearrange("(k p) n -> p k n", p=P)).then_inc(loaded, 16)
            for q in range(4):
                s = slice(4 * q, 4 * q + 4)
                sp.dma_start(m.X[:, s, :], a["x"][s].rearrange("b n d -> n b d")).then_inc(m.dma_x, 16)
            sp.dma_start(m.w_qkv1[:], a["L1_cond_W_qkv"].rearrange("(k p) n -> p k n", p=P)).then_inc(m.dma_w[0], 16)
            sp.dma_start(m.w_out1[:], a["L1_cond_W_out"].rearrange("(k p) n -> p k n", p=P)).then_inc(m.dma_w[0], 16)
            sp.dma_start(m.w_ih[:], a["L3_cond_W_ih"].rearrange("(k p) n -> p k n", p=P)).then_inc(m.dma_w[1], 16)
            big = m.big[:].rearrange("p (k n) -> p k n", k=KT)
            sp.dma_start(big, a["L2_cond_qkv_w"].rearrange("(k p) n -> p k n", p=P)).then_inc(m.dma_w[2], 16)

        @block.gpsimd
        def _(pool):
            c = Chain(pool, gstep)
            c.link(nc.gpsimd.memset(m.ident[:], 0.0))
            c.link(nc.gpsimd.memset(m.identb[:], 0.0))
            c.link(nc.gpsimd.memset(m.nhalf[:], -0.5))
            for t in (m.ident, m.identb):
                c.link(nc.gpsimd.affine_select(out=t[:], in_=t[:], compare_op=ALU.not_equal, fill=1.0, base=0,
                                               pattern=[[-1, P]], channel_multiplier=1))
            pool.wait_ge(loaded, 16 * 9)
            c.link(nc.gpsimd.tensor_copy(whp[:, 0], w_hh))
            c.link(nc.gpsimd.tensor_tensor(rest, w_hh, whp[:, 0], ALU.subtract))
            c.link(nc.gpsimd.tensor_copy(whp[:, 1], rest))
            nc.gpsimd.tensor_tensor(whp[:, 2], rest, whp[:, 1], ALU.subtract).then_inc(split, 1)

        @block.tensor
        def _(pe):
            pe.wait_ge(loaded, 16 * 9)
            for w, n, c0 in ((w_emb, 4, 0), (ada_w, 12, 4)):
                for c in range(n):
                    for k in range(KT):
                        mm = nc.tensor.matmul(m.ps[:, 0, (c0 + c) * B:(c0 + c + 1) * B], w[:, k, c * P:(c + 1) * P],
                                              m.condT[:, k, :], start=(k == 0), stop=(k == KT - 1))
            mm.then_inc(mod_ps, 1)

        @block.vector
        def _(dve):
            c = Chain(dve, vstep)
            dve.wait_ge(mod_ps, 1)
            dve.wait_ge(loaded, 16 * 9)
            mp = m.ps[:, 0, 0:256].rearrange("p (c b) -> p c b", b=B)
            c.link(nc.vector.tensor_tensor(m.mod1[:], mp[:, 0:4], bc(b_emb), ALU.add))
            c.link(nc.vector.tensor_tensor(m.ada[:], mp[:, 4:16], bc(ada_b), ALU.add))
            c.link(nc.vector.tensor_scalar(tmp, m.mod1[:, 0:2], 1.0, None, ALU.add))
            c.link(nc.vector.tensor_tensor(m.A1[:], tmp, bc(g_norm), ALU.mult))
            for g in (1, 4):
                s = m.ada[:, g * KT:(g + 1) * KT]
                c.link(nc.vector.tensor_scalar(s, s, 1.0, None, ALU.add))
            c.link(nc.vector.tensor_tensor(m.gb[:, 0:2], m.ada[:, 4:6], bc(out_b), ALU.mult))
            c.link(nc.vector.tensor_tensor(m.gb[:, 2:4], m.ada[:, 10:12], bc(ffn_b2), ALU.mult))


def phase_l0(nc, a, m, sem):
    q_st = m.ring[:, 0:4096].bitcast(BF16).rearrange("p (u h t) -> p u h t", u=2, h=H)
    k_st = m.ring[:, 4096:8192].bitcast(BF16).rearrange("p (u h t) -> p u h t", u=2, h=H)
    off = [0]

    def take(n, dt=F32):
        words = n if dt == F32 else n // 2
        v = m.work[:, off[0]:off[0] + words]
        off[0] += words
        return v if dt == F32 else v.bitcast(dt)

    xs = take(2 * D).rearrange("p (u t) -> p u t", u=2)
    mask = take(2 * D).rearrange("p (u t) -> p u t", u=2)
    w3 = take(3 * P).rearrange("p (g o) -> p g o", g=3)
    qk = take(2 * D)
    rest = take(2 * D)
    parts = take(NPART * 2 * D, BF16).rearrange("p (a n) -> p a n", a=NPART)
    vz = take(2 * 2 * 4 * VBLK).rearrange("p (u k j c) -> p u k j c", u=2, k=2, j=4)
    prob = take(2 * 2 * 2 * D).rearrange("p (a s q t) -> p a s q t", a=2, s=2, q=2)
    pts = take(2 * 4 * 2 * D).rearrange("p (a s n) -> p a s n", a=2, s=4)
    rrep = take(2 * P).rearrange("p (q c) -> p q c", q=2)
    rts = take(D)
    yn = take(D)
    sqx = take(D)
    bias32 = take(D)
    bias_r = take(D)
    bparts = take(NPART * D, BF16).rearrange("p (a n) -> p a n", a=NPART)
    nmax = m.cols[:, 0:8].rearrange("p (a s) -> p a s", a=2)
    rsum = m.cols[:, 16:80].rearrange("p (u q h) -> p u q h", u=2, q=2)
    rinv = m.cols[:, 96:128].rearrange("p (q h) -> p q h", q=2)
    b0 = m.cols[:, 128:129]
    scratch = nc.dram_tensor("qk_scratch", [2, 2, NPART, DH0, H, D], BF16, kind="Internal").ap()
    bias_d = nc.dram_tensor("bias_scratch", [B, NPART, D], BF16, kind="Internal").ap()
    names = ("l0_w_loaded l0_xs_loaded l0_bias_split l0_bias_stored l0_qk_proj l0_qk_evac l0_v_proj l0_v_evac "
             "l0_parts_ready l0_scr_written l0_stacks_loaded l0_scores_done l0_nmax_done l0_exp_done "
             "l0_pt_done l0_pts_ready l0_pv_done l0_rinv l0_rrep l0_rt_done l0_rts_ready l0_y_read l0_x1_done "
             "l0_gstep l0_ones l0_b_loaded").split()
    (w_loaded, xs_loaded, bias_split, bias_stored, qk_proj, qk_evac, v_proj, v_evac, parts_ready, scr_written,
     stacks_loaded, scores_done, nmax_done, exp_done, pt_done, pts_ready, pv_done, rinv_done, rrep_done,
     rt_done, rts_ready, y_read, x1_done, gstep, ones_done, b_loaded) = [sem(n) for n in names]
    SCALE0 = float(DH0) ** -0.5
    LOADS = 16 * (2 * NPART + 2)
    S_BANK, T_BANK, Y_BANK, J_BANK = 0, 4, 6, 7

    def bodies(eng, body):
        body(0, first=True)
        with eng.Fori(1, B // 2 - 1) as i:
            body(i)
        body(B // 2 - 1, last=True)

    with nc.Block() as block:
        @block.sync
        def _(sp):
            for g, n in enumerate(("WqT", "WkT", "WvT")):
                sp.dma_start(w3[:, g], a[n]).then_inc(w_loaded, 16)
            sp.dma_start(bias32[0:B, :], a["cond_2048"]).then_inc(b_loaded, 16)
            sp.dma_start(b0[0:B, :], a["L0_cond_b"].unsqueeze(0).broadcast_to([B, 1])).then_inc(b_loaded, 16)
            sp.wait_ge(bias_split, 1)
            sp.dma_start(bias_d, bparts[0:B]).then_inc(bias_stored, 16)
            sp.wait_ge(bias_stored, 16)
            sp.wait_ge(ones_done, 1)

            def prep(b, u):
                sp.dma_start(xs[:, u], a["x"][bass.ds(b, 1)].rearrange("o c t -> c (o t)")).then_inc(xs_loaded, 16)
                sp.dma_start(mask[:, u], a["cond_2048"][bass.ds(b, 1)].broadcast_to([P, D])).then_inc(xs_loaded, 16)
                sp.wait_ge(parts_ready, b + 1)
                carry(sp, m)
                for j in range(NPART):
                    for g in range(2):
                        sp.dma_start(scratch[u, g, j].rearrange("d h t -> h d t"),
                                     parts[:, j, g * D:(g + 1) * D]).then_inc(scr_written, 16)
                sp.wait_ge(scr_written, 96 * (b + 1))
                carry(sp, m)
                for i in range(NPART):
                    sp.dma_start(q_st[24 * i:24 * i + 24, u].rearrange("p h t -> p (h t)"),
                                 scratch[u, 0, i].rearrange("d h t -> d (h t)").unsqueeze(0).broadcast_to([NPART, DH0, H * D])
                                 ).then_inc(stacks_loaded, 16)
                    sp.dma_start(k_st[24 * i:24 * i + 24, u].rearrange("p h t -> p (h t)"),
                                 scratch[u, 1].rearrange("a d h t -> (a d) (h t)")).then_inc(stacks_loaded, 16)
                for hh in range(2):
                    sp.dma_start(k_st[TERMS:ROWS0, u, 8 * hh:8 * hh + 8],
                                 bias_d[bass.ds(b, 1)].rearrange("o a t -> (o a) t").unsqueeze(1).broadcast_to([NPART, 8, D])
                                 ).then_inc(stacks_loaded, 16)

            prep(0, 0)
            prep(1, 1)
            with sp.Fori(1, B // 2) as i:
                for u in range(2):
                    sp.wait_ge(v_proj, 2 * i + u - 1)
                    carry(sp, m)
                    sp.wait_ge(scores_done, PAIRS * (2 * i + u - 1))
                    carry(sp, m)
                    prep(2 * i + u, u)
            sp.wait_ge(scores_done, PAIRS * B)
            w = m.ring
            sp.dma_start(w[:, 0:4096].rearrange("p (k n) -> p k n", k=H),
                         a["L2_cond_out_w"].rearrange("(k p) n -> p k n", p=P)).then_inc(m.dma_w[3], 16)
            sp.dma_start(w[:, 4096:6144].rearrange("p (k n) -> p k n", k=KT),
                         a["L2_cond_ffn_w1"].rearrange("(k p) n -> p k n", p=P)).then_inc(m.dma_w[3], 16)
            sp.dma_start(w[:, 6144:8192].rearrange("p (k n) -> p k n", k=8),
                         a["L2_cond_ffn_w2"].rearrange("(k p) n -> p k n", p=P)).then_inc(m.dma_w[3], 16)

        @block.tensor
        def _(pe):
            pe.sem_inc(pt_done, 2)
            pe.sem_inc(pv_done, 2)
            pe.wait_ge(w_loaded, 48)

            def proj_qk(b, u):
                pe.wait_ge(xs_loaded, 32 * (b + 1))
                pe.wait_ge(v_evac, b)
                for g in range(2):
                    mm = nc.tensor.matmul(m.ps[:, J_BANK, g * D:(g + 1) * D], w3[:, g], xs[:, u], start=True, stop=True)
                mm.then_inc(qk_proj, 1)

            def proj_v(b, u):
                pe.wait_ge(qk_evac, b + 1)
                for k in range(2):
                    mm = nc.tensor.matmul(m.ps[:, J_BANK, k * P:(k + 1) * P], xs[:, u, k * P:(k + 1) * P], w3[:, 2],
                                          start=True, stop=True)
                mm.then_inc(v_proj, 1)

            def scores(b, u, p):
                if p == 0:
                    pe.wait_ge(stacks_loaded, LOADS * (b + 1))
                for s in range(2):
                    h = ORDER0[2 * p + s]
                    for q in range(2):
                        mm = nc.tensor.matmul(m.ps[:, S_BANK + 2 * (p % 2) + s, q * D:(q + 1) * D],
                                              q_st[0:ROWS0, u, h, q * P:(q + 1) * P], k_st[0:ROWS0, u, h],
                                              start=True, stop=True)
                mm.then_inc(scores_done, 1)

            def turn(b, u, p):
                pe.wait_ge(exp_done, PAIRS * b + p + 1)
                pe.wait_ge(pts_ready, PAIRS * b + p)
                for s in range(2):
                    for k in range(2):
                        for q in range(2):
                            mm = nc.tensor.transpose(m.ps[:, T_BANK + s, k * D + q * P:k * D + (q + 1) * P],
                                                     prob[:, p % 2, s, q, k * P:(k + 1) * P], m.ident[:])
                mm.then_inc(pt_done, 1)

            def pv(b, u, g):
                if g == 0:
                    pe.wait_ge(y_read, b)
                    pe.wait_ge(v_evac, b + 1)
                pe.wait_ge(pts_ready, PAIRS * b + 2 * g + 2)
                for k in range(2):
                    for j in range(4):
                        mm = nc.tensor.matmul(m.ps[32 * j:32 * j + 32, Y_BANK, 0:D], vz[:, u, k, j, 32 * g:32 * g + 32],
                                              pts[:, g % 2, j, k * D:(k + 1) * D],
                                              start=(g == 0 and k == 0), stop=(g == 3 and k == 1),
                                              tile_position=(0, 32 * j))
                mm.then_inc(pv_done, 1)

            def recip_turn(b):
                pe.wait_ge(rrep_done, b + 1)
                for q in range(2):
                    mm = nc.tensor.transpose(m.ps[:, Y_BANK, D + q * P:D + (q + 1) * P], rrep[:, q], m.ident[:])
                mm.then_inc(rt_done, 1)

            proj_qk(0, 0)
            proj_v(0, 0)
            scores(0, 0, 0)
            scores(0, 0, 1)

            def body(i, first=False, last=False):
                for u in range(2):
                    b = 2 * i + u
                    for p in range(PAIRS):
                        turn(b, u, p)
                        if p < PAIRS - 2:
                            scores(b, u, p + 2)
                        elif not (last and u == 1):
                            scores(b + 1, 1 - u, p + 2 - PAIRS)
                        if p == 0 and not (first and u == 0):
                            recip_turn(b - 1)
                        if p == 0 and not (last and u == 1):
                            proj_qk(b + 1, 1 - u)
                        if p == 1 and not (last and u == 1):
                            proj_v(b + 1, 1 - u)
                        if p % 2:
                            pv(b, u, p // 2)

            bodies(pe, body)
            recip_turn(B - 1)

        @block.scalar
        def _(act):
            def exps(b, u, p):
                act.wait_ge(nmax_done, PAIRS * b + p + 1)
                act.wait_ge(pt_done, PAIRS * b + p + 1)
                for s in range(2):
                    h = ORDER0[2 * p + s]
                    for q in range(2):
                        ins = nc.scalar.activation(prob[:, p % 2, s, q], m.ps[:, S_BANK + 2 * (p % 2) + s, q * D:(q + 1) * D],
                                                   ACT.Exp, bias=nmax[:, p % 2, 2 * s + q:2 * s + q + 1],
                                                   accum_out=rsum[:, u, q, h:h + 1])
                ins.then_inc(exp_done, 1)

            def recip_copy(b):
                act.wait_ge(rt_done, b + 1)
                act.wait_ge(y_read, b)
                nc.scalar.activation(rts, m.ps[:, Y_BANK, D:2 * D], ACT.Copy).then_inc(rts_ready, 1)

            def square(b):
                act.wait_ge(x1_done, b + 1)
                nc.scalar.activation(sqx, row(m.X, b), ACT.Square, accum_out=m.ssq[:, bass.ds(b, 1)])

            def body(i, first=False, last=False):
                for u in range(2):
                    b = 2 * i + u
                    for p in range(PAIRS):
                        exps(b, u, p)
                        if p == 1 and not (first and u == 0):
                            recip_copy(b - 1)
                        if p == 5 and not (first and u == 0):
                            square(b - 1)

            bodies(act, body)
            recip_copy(B - 1)
            square(B - 1)

        @block.vector
        def _(dve):
            for u in range(2):
                nc.vector.memset(vz[:, u], 0.0)
                nc.vector.memset(q_st[64:96, u], 1.0)
            dve.drain().then_inc(ones_done, 1)
            dve.wait_ge(ones_done, 1)

            def evac_qk(b, u):
                dve.wait_ge(qk_proj, b + 1)
                dve.wait_ge(parts_ready, b)
                nc.vector.tensor_copy(qk[:, 0:D], m.ps[:, J_BANK, 0:D])
                nc.vector.scalar_tensor_tensor(out=qk[:, D:2 * D], in0=m.ps[:, J_BANK, D:2 * D], scalar=SCALE0,
                                               in1=mask[:, u], op0=ALU.mult, op1=ALU.mult).then_inc(qk_evac, 1)

            def evac_v(b, u):
                dve.wait_ge(v_proj, b + 1)
                if not (type(b) is int and b == 0):
                    dve.wait_ge(pv_done, 4 * (b - 1) + 2)
                nc.vector.tensor_copy(vz[:, u].rearrange("p k j (r c) -> p (k j) r c", c=40)[:, :, :, 0:DH0],
                                      m.ps[:, J_BANK, 0:D].rearrange("p (a r c) -> p a r c", a=8, c=DH0)).then_inc(v_evac, 1)

            def maxes(b, p):
                dve.wait_ge(scores_done, PAIRS * b + p + 1)
                k = S_BANK + 2 * (p % 2)
                nc.vector.tensor_reduce(nmax[:, p % 2], m.ps[:, k:k + 2].rearrange("p s (q t) -> p (s q) t", q=2),
                                        AX.X, ALU.max, negate=True).then_inc(nmax_done, 1)

            def evac_pt(b, p):
                dve.wait_ge(pt_done, PAIRS * b + p + 3)
                if p % 2 == 0:
                    dve.wait_ge(pv_done, 4 * b + p // 2 + 1)
                s = 2 * (p % 2)
                nc.vector.tensor_copy(pts[:, (p // 2) % 2, s:s + 2], m.ps[:, T_BANK:T_BANK + 2]).then_inc(pts_ready, 1)

            def recip(b, u):
                dve.wait_ge(exp_done, PAIRS * (b + 1))
                nc.vector.reciprocal(rinv, rsum[:, u]).then_inc(rinv_done, 1)

            def norm(b):
                dve.wait_ge(rts_ready, b + 1)
                dve.wait_ge(x1_done, b)
                nc.vector.tensor_tensor(yn, m.ps[:, Y_BANK, 0:D], rts, ALU.mult).then_inc(y_read, 1)

            evac_qk(0, 0)
            evac_v(0, 0)
            maxes(0, 0)

            def body(i, first=False, last=False):
                for u in range(2):
                    b = 2 * i + u
                    for p in range(PAIRS):
                        if p < PAIRS - 1:
                            maxes(b, p + 1)
                        elif not (last and u == 1):
                            maxes(b + 1, 0)
                        if p == 0 and not (first and u == 0):
                            recip(b - 1, 1 - u)
                        evac_pt(b, p)
                        if p == 1 and not (first and u == 0):
                            norm(b - 1)
                        if p == 0 and not (last and u == 1):
                            evac_qk(b + 1, 1 - u)
                        if p == 2 and not (last and u == 1):
                            evac_v(b + 1, 1 - u)

            bodies(dve, body)
            recip(B - 1, 1)
            norm(B - 1)

        @block.gpsimd
        def _(pool):
            c = Chain(pool, gstep)
            pool.wait_ge(b_loaded, 32)
            c.link(nc.gpsimd.tensor_scalar(bias_r[0:B], bias32[0:B], -NEG, NEG, ALU.mult, ALU.add))
            c.link(nc.gpsimd.tensor_scalar(bias32[0:B], bias32[0:B], b0[0:B], None, ALU.mult))
            c.link(nc.gpsimd.tensor_tensor(bias32[0:B], bias32[0:B], bias_r[0:B], ALU.add))
            c.link(nc.gpsimd.tensor_copy(bparts[0:B, 0], bias32[0:B]))
            c.link(nc.gpsimd.tensor_tensor(bias_r[0:B], bias32[0:B], bparts[0:B, 0], ALU.subtract))
            c.link(nc.gpsimd.tensor_copy(bparts[0:B, 1], bias_r[0:B]))
            nc.gpsimd.tensor_tensor(bparts[0:B, 2], bias_r[0:B], bparts[0:B, 1], ALU.subtract).then_inc(bias_split, 1)
            base = c.n
            pool.wait_ge(m.dma_x, 64)

            def split(b):
                c = Chain(pool, gstep, base + 3 * b)
                pool.wait_ge(qk_evac, b + 1)
                pool.wait_ge(scr_written, 96 * b)
                carry(pool, m)
                c.link(nc.gpsimd.tensor_copy(parts[:, 0], qk))
                c.link(nc.gpsimd.tensor_tensor(rest, qk, parts[:, 0], ALU.subtract))
                carry(pool, m)
                c.link(nc.gpsimd.tensor_copy(parts[:, 1], rest))
                nc.gpsimd.tensor_tensor(parts[:, 2], rest, parts[:, 1], ALU.subtract).then_inc(parts_ready, 1)

            def spread(b):
                pool.wait_ge(rinv_done, b + 1)
                pool.wait_ge(rt_done, b)
                carry(pool, m)
                nc.gpsimd.tensor_copy(rrep.rearrange("p q (h d) -> p q h d", d=DH0),
                                      rinv.unsqueeze(3).broadcast_to([P, 2, H, DH0])).then_inc(rrep_done, 1)

            def add(b):
                pool.wait_ge(y_read, b + 1)
                x = m.X[:, bass.ds(b, 1), :].rearrange("p o t -> p (o t)")
                nc.gpsimd.tensor_tensor(x, x, yn, ALU.add).then_inc(x1_done, 1)

            split(0)
            def body(i, first=False, last=False):
                for u in range(2):
                    b = 2 * i + u
                    if not (first and u == 0):
                        spread(b - 1)
                    if not (last and u == 1):
                        split(b + 1)
                    if not (first and u == 0):
                        add(b - 1)

            bodies(pool, body)
            spread(B - 1)
            add(B - 1)


class Space:

    def __init__(self, tile):
        self.tile, self.at = tile, 0

    def take(self, n, dt=F32):
        words = n if dt == F32 else n // 2
        v = self.tile[:, self.at:self.at + words]
        self.at += words
        return v if dt == F32 else v.bitcast(dt)


def row(t, b):
    return t[:, bass.ds(b, 1), :].rearrange("p o n -> p (o n)")


def col(t, c, b):
    return t[:, c, bass.ds(b, 1)]


def phase_l1(nc, a, m, sem):
    w = Space(m.work)
    xn = w.take(D)
    xnT = w.take(2 * KT * P).rearrange("p (u k t) -> p u k t", u=2, k=KT)
    sq = w.take(2 * D)
    qkn = w.take(2 * D)
    qT = w.take(2 * 2 * P).rearrange("p (u g t) -> p u g t", u=2, g=2)
    kz = w.take(2 * 8 * P * 2).rearrange("p (g h t) -> p g h t", g=2, h=8)[:, :, :, :]
    kz = kz.rearrange("p g h (u t) -> p u g h t", u=2)
    vz = w.take(2 * 8 * 64).rearrange("p (u j c) -> p u j c", u=2, j=8)
    prob = w.take(2 * 512).rearrange("p (a n) -> p a n", a=2)
    pts = w.take(2 * 512).rearrange("p (a n) -> p a n", a=2)
    rrep = w.take(D)
    rts = w.take(D)
    oraw = w.take(D)
    oT = w.take(D).rearrange("p (g t) -> p g t", g=2)
    raw = w.take(2 * 2 * D).rearrange("p (u n) -> p u n", u=2)
    msq, rx = m.cols[:, 0:B], m.cols[:, B:2 * B]
    ssk = m.cols[:, 32:64]
    msk = m.cols[:, 224:288].rearrange("p (u h) -> p u h", u=2)
    rqk = m.cols[:, 64:128].rearrange("p (u h) -> p u h", u=2)
    nmax = m.cols[:, 128:136].rearrange("p (a h) -> p a h", a=2)
    rsum = m.cols[:, 160:192].rearrange("p (u h) -> p u h", u=2)
    rinv = m.cols[:, 192:208]
    gq = m.cols[:, 208:209]
    gk = m.cols[:, 209:210]
    hmask = m.cols[:, 216:224]
    names = ("l1_g_loaded l1_set l1_raw l1_msq l1_rx l1_xn l1_xnT_ps l1_xnT l1_qk_ps l1_msk l1_rqk l1_qkn "
             "l1_qkT_ps l1_kz l1_v_ps l1_v l1_scores l1_nmax l1_exp l1_pt_ps l1_pts l1_pv l1_oraw l1_rinv l1_rrep "
             "l1_rt_ps l1_rts l1_oT l1_out_ps l1_x l1_vstep l1_gstep").split()
    (g_loaded, set_done, raw_s, msq_s, rx_s, xn_s, xnT_ps, xnT_s, qk_ps, msk_s, rqk_s, qkn_s, qkT_ps, kz_s,
     v_ps, v_s, scores_s, nmax_s, exp_s, pt_ps, pts_s, pv_s, oraw_s, rinv_s, rrep_s, rt_ps, rts_s, oT_s, out_ps, x_s,
     vstep, gstep) = [sem(n) for n in names]
    QK, VB, KTB, SB, TB, OB, RB = 0, 1, 2, 3, 5, 6, 7
    bank = lambda k, lo=0, hi=512: m.ps[:, k, lo:hi]
    head = lambda n, j: 8 * (n // 2) + 2 * j + n % 2

    def bodies(eng, body):
        body(0, first=True)
        with eng.Fori(1, B // 2 - 1) as i:
            body(i)
        body(B // 2 - 1, last=True)

    with nc.Block() as block:
        @block.sync
        def _(sp):
            for g in range(8):
                sp.dma_start(gq[DH1 * g:DH1 * g + DH1, :], a["L1_cond_g_q"].unsqueeze(1)).then_inc(g_loaded, 16)
                sp.dma_start(gk[DH1 * g:DH1 * g + DH1, :], a["L1_cond_g_k"].unsqueeze(1)).then_inc(g_loaded, 16)

        @block.tensor
        def _(pe):
            pe.sem_inc(pt_ps, 2)
            pe.sem_inc(pv_s, 2)
            pe.wait_ge(m.dma_w[0], 32)

            def turn_x(c):
                pe.wait_ge(xn_s, c + 1)
                if type(c) is int and c < 2:
                    pe.wait_ge(v_s, c)
                else:
                    pe.wait_ge(v_s, c - 1)
                for k in range(KT):
                    mm = nc.tensor.transpose(bank(VB, D + k * P, D + (k + 1) * P), xn[:, k * P:(k + 1) * P], m.ident[:])
                mm.then_inc(xnT_ps, 1)

            def proj_qk(c, u):
                pe.wait_ge(xnT_s, c + 1)
                pe.wait_ge(raw_s, c)
                for k in range(KT):
                    mm = nc.tensor.matmul(bank(QK), xnT[:, u, k], m.w_qkv1[:, k, 0:2 * D], start=(k == 0), stop=(k == KT - 1))
                mm.then_inc(qk_ps, 1)

            def proj_v(c, u, turned):
                pe.wait_ge(xnT_s, turned)
                for k in range(KT):
                    mm = nc.tensor.matmul(bank(VB, 0, D), xnT[:, u, k], m.w_qkv1[:, k, 2 * D:3 * D],
                                          start=(k == 0), stop=(k == KT - 1))
                mm.then_inc(v_ps, 1)

            def turn_qk(c):
                pe.wait_ge(qkn_s, c + 1)
                pe.wait_ge(kz_s, 2 * c)
                for g in range(4):
                    mm = nc.tensor.transpose(bank(KTB, g * P, (g + 1) * P), qkn[:, g * P:(g + 1) * P], m.ident[:])
                mm.then_inc(qkT_ps, 1)

            def scores(c, u, n):
                if n % 2 == 0:
                    pe.wait_ge(kz_s, 2 * c + 1 + n // 2)
                mm = nc.tensor.matmul(bank(SB + n % 2), qT[:, u, n // 2], kz[:, u, n // 2, n % 2:8:2, :], start=True, stop=True)
                mm.then_inc(scores_s, 1)

            def turn_p(c, n):
                pe.wait_ge(exp_s, 4 * c + n + 1)
                pe.wait_ge(pts_s, 4 * c + n)
                for j in range(4):
                    mm = nc.tensor.transpose(bank(TB, j * P, (j + 1) * P), prob[:, n % 2, j * P:(j + 1) * P], m.ident[:])
                mm.then_inc(pt_ps, 1)

            def pv(c, u, n):
                if n == 0:
                    pe.wait_ge(v_s, c + 1)
                    pe.wait_ge(oraw_s, c)
                pe.wait_ge(pts_s, 4 * c + n + 1)
                for j in range(4):
                    h = head(n, j)
                    g = n // 2
                    mm = nc.tensor.matmul(m.ps[32 * j:32 * j + 32, OB, g * P:(g + 1) * P],
                                          vz[:, u, h // 2, 32 * (h % 2):32 * (h % 2) + 32], pts[:, n % 2, j * P:(j + 1) * P],
                                          start=(n % 2 == 0), stop=(n % 2 == 1), tile_position=(0, 32 * j))
                mm.then_inc(pv_s, 1)

            def turn_r(c):
                pe.wait_ge(rrep_s, c + 1)
                pe.wait_ge(x_s, c)
                for g in range(2):
                    mm = nc.tensor.transpose(bank(RB, g * P, (g + 1) * P), rrep[:, g * P:(g + 1) * P], m.ident[:])
                mm.then_inc(rt_ps, 1)

            def out_proj(c):
                pe.wait_ge(oT_s, c + 1)
                nc.tensor.matmul(bank(RB, D, 2 * D), oT[:, 0], m.w_out1[:, 0], start=True, stop=False)
                for g in range(2):
                    nc.tensor.matmul(bank(RB, D + g * P, D + (g + 1) * P), oT[:, g], m.ident[:], start=False, stop=False,
                                     skip_group_check=True)
                mm = nc.tensor.matmul(bank(RB, D, 2 * D), oT[:, 1], m.w_out1[:, 1], start=False, stop=True)
                mm.then_inc(out_ps, 1)

            def stage_a(c, u):
                turn_x(c)
                proj_qk(c, u)

            stage_a(0, 0)
            proj_v(0, 0, 1)
            stage_a(1, 1)
            turn_qk(0)
            scores(0, 0, 0)
            scores(0, 0, 1)

            def body(i, first=False, last=False):
                for u in range(2):
                    b = 2 * i + u
                    head_, tail = first and u == 0, last and u == 1
                    for n in range(4):
                        turn_p(b, n)
                        if n == 0 and not last:
                            turn_x(b + 2)
                        if n == 1 and not head_:
                            turn_r(b - 1)
                        if n < 2:
                            scores(b, u, n + 2)
                        elif not tail:
                            scores(b + 1, 1 - u, n - 2)
                        if n == 1 and not tail:
                            turn_qk(b + 1)
                        if n == 3 and not head_:
                            out_proj(b - 1)
                        pv(b, u, n)
                        if n == 0 and not last:
                            proj_qk(b + 2, u)
                        if n == 1 and not tail:
                            proj_v(b + 1, 1 - u, B if last else b + 3)

            bodies(pe, body)
            turn_r(B - 1)
            out_proj(B - 1)

        @block.scalar
        def _(act):
            def copy_qk(c, u):
                act.wait_ge(qk_ps, c + 1)
                if not (type(c) is int and c < 2):
                    act.wait_ge(qkn_s, c - 1)
                act.wait_ge(msk_s, c)
                nc.scalar.activation(raw[:, u], bank(QK), ACT.Copy)
                nc.scalar.activation(sq, bank(QK), ACT.Square).then_inc(raw_s, 1)

            def copy_v(c, u):
                act.wait_ge(v_ps, c + 1)
                act.wait_ge(set_done, 4)
                src = bank(VB, 0, D).rearrange("p (j r c) -> p j r c", j=8, r=2)
                nc.scalar.activation(vz[:, u, :, 0:DH1], src[:, :, 0], ACT.Copy)
                nc.scalar.activation(vz[:, u, :, 48:48 + DH1], src[:, :, 1], ACT.Copy).then_inc(v_s, 1)

            def exps(c, u, n):
                act.wait_ge(nmax_s, 4 * c + n + 1)
                act.wait_ge(pt_ps, 4 * c + n + 1)
                for j in range(4):
                    h = head(n, j)
                    ins = nc.scalar.activation(prob[:, n % 2, j * P:(j + 1) * P], bank(SB + n % 2, j * P, (j + 1) * P),
                                               ACT.Exp, bias=nmax[:, n % 2, j:j + 1], accum_out=rsum[:, u, h:h + 1])
                ins.then_inc(exp_s, 1)

            def copy_pt(c, n):
                act.wait_ge(pt_ps, 4 * c + n + 3)
                act.wait_ge(pv_s, 4 * c + n + 1)
                nc.scalar.activation(pts[:, n % 2], bank(TB), ACT.Copy).then_inc(pts_s, 1)

            def copy_r(c):
                act.wait_ge(rt_ps, c + 1)
                act.wait_ge(oT_s, c)
                nc.scalar.activation(rts, bank(RB, 0, D), ACT.Copy).then_inc(rts_s, 1)

            copy_qk(0, 0)
            copy_v(0, 0)
            copy_qk(1, 1)
            exps(0, 0, 0)

            def body(i, first=False, last=False):
                for u in range(2):
                    b = 2 * i + u
                    head_, tail = first and u == 0, last and u == 1
                    for n in range(4):
                        if n < 3:
                            exps(b, u, n + 1)
                        elif not tail:
                            exps(b + 1, 1 - u, 0)
                        if n == 1 and not last:
                            copy_qk(b + 2, u)
                        copy_pt(b, n)
                        if n == 1 and not head_:
                            copy_r(b - 1)
                        if n == 2 and not tail:
                            copy_v(b + 1, 1 - u)

            bodies(act, body)
            copy_r(B - 1)

        @block.vector
        def _(dve):
            for u in range(2):
                nc.vector.memset(vz[:, u], 0.0).then_inc(set_done, 1)
            dve.wait_ge(g_loaded, 16 * 16)
            dve.wait_ge(set_done, 3)
            nc.vector.tensor_scalar(gq, gq, float(DH1) ** -0.5, None, ALU.mult).then_inc(set_done, 1)
            nc.vector.tensor_scalar(hmask, hmask, gk, None, ALU.mult).then_inc(vstep, 1)
            dve.wait_ge(set_done, 4)
            dve.wait_ge(vstep, 1)

            def mean_x(c0, c1, k):
                nc.vector.tensor_scalar(msq[:, c0:c1], m.ssq[:, c0:c1], 1.0 / D, EPS, ALU.mult, ALU.add).then_inc(msq_s, 1)

            def norm_x(c):
                dve.wait_ge(xnT_ps, c)
                nc.vector.tensor_scalar(xn, row(m.X, c), rx[:, bass.ds(c, 1)], None, ALU.mult).then_inc(xn_s, 1)

            def modulate(c, u):
                dve.wait_ge(xnT_ps, c + 1)
                for k in range(KT):
                    ins = nc.vector.tensor_scalar(xnT[:, u, k], bank(VB, D + k * P, D + (k + 1) * P), col(m.A1, k, c),
                                                  col(m.mod1, KT + k, c), ALU.mult, ALU.add)
                ins.then_inc(xnT_s, 1)

            def mean_qk(c, u):
                dve.wait_ge(raw_s, c + 1)
                if not (type(c) is int and c < 2):
                    dve.wait_ge(rqk_s, c - 1)
                nc.vector.tensor_reduce(ssk, sq.rearrange("p (h d) -> p h d", d=DH1), AX.X, ALU.add).then_inc(vstep, 1)
                dve.wait_ge(vstep, c + 2)
                nc.vector.tensor_scalar(msk[:, u], ssk, 1.0 / DH1, EPS, ALU.mult, ALU.add).then_inc(msk_s, 1)

            def norm_qk(c, u):
                dve.wait_ge(rqk_s, c + 1)
                dve.wait_ge(qkT_ps, c)
                nc.vector.tensor_tensor(qkn.rearrange("p (h d) -> p h d", d=DH1), raw[:, u].rearrange("p (h d) -> p h d", d=DH1),
                                        rqk[:, u].unsqueeze(2).broadcast_to([P, 2 * H, DH1]), ALU.mult).then_inc(qkn_s, 1)

            def spread_q(c, u):
                dve.wait_ge(qkT_ps, c + 1)
                nc.vector.tensor_scalar(qT[:, u], bank(KTB, 0, 2 * P).rearrange("p (g t) -> p g t", g=2), gq, None, ALU.mult)

            def spread_k(c, u, g):
                nc.vector.tensor_tensor(kz[:, u, g], bank(KTB, (2 + g) * P, (3 + g) * P).unsqueeze(1).broadcast_to([P, 8, P]),
                                        hmask.unsqueeze(2).broadcast_to([P, 8, P]), ALU.mult).then_inc(kz_s, 1)

            def maxes(c, n):
                dve.wait_ge(scores_s, 4 * c + n + 1)
                nc.vector.tensor_reduce(nmax[:, n % 2], bank(SB + n % 2).rearrange("p (h t) -> p h t", h=4), AX.X, ALU.max,
                                        negate=True).then_inc(nmax_s, 1)

            def recip(c, u):
                dve.wait_ge(exp_s, 4 * (c + 1))
                dve.wait_ge(rrep_s, c)
                nc.vector.reciprocal(rinv, rsum[:, u]).then_inc(rinv_s, 1)

            def take_o(c):
                dve.wait_ge(pv_s, 4 * (c + 1) + 2)
                dve.wait_ge(oT_s, c)
                nc.vector.tensor_copy(oraw, bank(OB, 0, D)).then_inc(oraw_s, 1)

            def norm_o(c):
                dve.wait_ge(rts_s, c + 1)
                dve.wait_ge(oraw_s, c + 1)
                dve.wait_ge(out_ps, c)
                nc.vector.tensor_tensor(oT.rearrange("p g t -> p (g t)"), oraw, rts, ALU.mult).then_inc(oT_s, 1)

            def add(c):
                dve.wait_ge(out_ps, c + 1)
                nc.vector.tensor_tensor(row(m.X, c), row(m.X, c), bank(RB, D, 2 * D), ALU.add).then_inc(x_s, 1)

            mean_x(0, 2, 0)
            mean_x(2, B, 1)
            dve.wait_ge(rx_s, 1)
            norm_x(0)
            modulate(0, 0)
            norm_x(1)
            modulate(1, 1)
            mean_qk(0, 0)
            mean_qk(1, 1)
            norm_qk(0, 0)
            spread_q(0, 0)
            spread_k(0, 0, 0)
            spread_k(0, 0, 1)
            maxes(0, 0)
            dve.wait_ge(rx_s, 2)

            def body(i, first=False, last=False):
                for u in range(2):
                    b = 2 * i + u
                    head_, tail = first and u == 0, last and u == 1
                    for n in range(4):
                        if n < 3:
                            maxes(b, n + 1)
                        elif not tail:
                            maxes(b + 1, 0)
                        if n == 0 and not last:
                            norm_x(b + 2)
                        if n == 0 and not head_:
                            recip(b - 1, 1 - u)
                        if n == 0 and not first:
                            add(b - 2)
                        if n == 0 and not last:
                            modulate(b + 2, u)
                        if n == 0 and not head_:
                            take_o(b - 1)
                        if n == 1 and not tail:
                            norm_qk(b + 1, 1 - u)
                        if n == 1 and not tail:
                            spread_q(b + 1, 1 - u)
                            spread_k(b + 1, 1 - u, 0)
                        if n == 2 and not last:
                            mean_qk(b + 2, u)
                        if n == 2 and not tail:
                            spread_k(b + 1, 1 - u, 1)
                        if n == 2 and not head_:
                            norm_o(b - 1)

            bodies(dve, body)
            recip(B - 1, 1)
            take_o(B - 1)
            add(B - 2)
            norm_o(B - 1)
            add(B - 1)

        @block.gpsimd
        def _(pool):
            c = Chain(pool, gstep)
            c.link(nc.gpsimd.memset(hmask, 1.0))
            c.link(nc.gpsimd.affine_select(out=hmask, in_=hmask, compare_op=ALU.is_ge, fill=0.0, base=0,
                                           pattern=[[-DH1, 8]], channel_multiplier=1))
            nc.gpsimd.affine_select(out=hmask, in_=hmask, compare_op=ALU.is_ge, fill=0.0, base=DH1 - 1,
                                    pattern=[[DH1, 8]], channel_multiplier=-1).then_inc(set_done, 1)

            def pow_x(c0, c1, k):
                pool.wait_ge(msq_s, k + 1)
                nc.gpsimd.tensor_tensor(rx[:, c0:c1], msq[:, c0:c1], m.nhalf[:, c0:c1], ALU.pow).then_inc(rx_s, 1)

            def pow_qk(c, u):
                pool.wait_ge(msk_s, c + 1)
                if not (type(c) is int and c < 2):
                    pool.wait_ge(qkn_s, c - 1)
                nc.gpsimd.tensor_tensor(rqk[:, u], msk[:, u], m.nhalf[:], ALU.pow).then_inc(rqk_s, 1)

            def spread(c):
                pool.wait_ge(rinv_s, c + 1)
                pool.wait_ge(rt_ps, c)
                carry(pool, m)
                nc.gpsimd.tensor_copy(rrep.rearrange("p (h d) -> p h d", d=DH1),
                                      rinv.unsqueeze(2).broadcast_to([P, H, DH1])).then_inc(rrep_s, 1)

            pow_x(0, 2, 0)
            pow_qk(0, 0)
            pow_qk(1, 1)
            pow_x(2, B, 1)

            def body(i, first=False, last=False):
                for u in range(2):
                    b = 2 * i + u
                    head_ = first and u == 0
                    if not head_:
                        spread(b - 1)
                    if not last:
                        pow_qk(b + 2, u)

            bodies(pool, body)
            spread(B - 1)


def phase_l2(nc, a, m, sem):
    w = Space(m.work)
    xn = w.take(D)
    x1T = w.take(KT * P).rearrange("p (k t) -> p k t", k=KT)
    qT = w.take(4 * P).rearrange("p (h t) -> p h t", h=4)
    kT = w.take(4 * P).rearrange("p (h t) -> p h t", h=4)
    vv = w.take(2 * 4 * P).rearrange("p (a n) -> p a n", a=2)
    prob = w.take(4 * P).rearrange("p (h t) -> p h t", h=4)
    pn = w.take(4 * P).rearrange("p (h t) -> p h t", h=4)
    pts = w.take(4 * P).rearrange("p (h t) -> p h t", h=4)
    oT = w.take(4 * P).rearrange("p (h t) -> p h t", h=4)
    ao = w.take(KT * P).rearrange("p (k t) -> p k t", k=KT)
    stats = m.cols[:, 0:6]
    mv = m.cols[:, 8:10]
    var, rstd = m.cols[:, 10:11], m.cols[:, 11:12]
    nmax = m.cols[:, 16:20]
    rsum = m.cols[:, 24:28]
    rinv = m.cols[:, 32:36]
    bq = m.cols[:, 64:112]
    wqkv = m.big[:].rearrange("p (k g n) -> p k g n", k=KT, g=3)
    wo = m.ring[:, 0:4096].rearrange("p (h n) -> p h n", h=H)
    names = ("l2_b_loaded l2_var l2_rstd l2_xn l2_xT_ps l2_x1T l2_q_ps l2_k_ps l2_v_ps l2_q l2_k l2_v l2_scores "
             "l2_nmax l2_exp l2_rinv l2_pn l2_pt_ps l2_pts l2_pv l2_oT l2_out_ps l2_ao l2_back_ps l2_x l2_vstep").split()
    (b_loaded, var_s, rstd_s, xn_s, xT_ps, x1T_s, q_ps, k_ps, v_ps, q_s, k_s, v_s, scores_s, nmax_s, exp_s, rinv_s,
     pn_s, pt_ps, pts_s, pv_s, oT_s, out_ps, ao_s, back_ps, x_s, vstep) = [sem(n) for n in names]
    QB, KB, VB, SB, TB, OB, AB = 0, 1, 2, 3, 4, 5, 6
    bank = lambda k, lo=0, hi=512: m.ps[:, k, lo:hi]
    four = lambda v: v.rearrange("p (h t) -> p h t", h=4)

    def bodies(eng, body):
        body(0, first=True)
        with eng.Fori(1, B - 1) as b:
            body(b)
        body(B - 1, last=True)

    with nc.Block() as block:
        @block.sync
        def _(sp):
            sp.dma_start(bq, a["col_L2_cond_qkv_b"]).then_inc(b_loaded, 16)

        @block.tensor
        def _(pe):
            def turn_x(c):
                pe.wait_ge(xn_s, c + 1)
                for k in range(KT):
                    mm = nc.tensor.transpose(bank(SB, k * P, (k + 1) * P), xn[:, k * P:(k + 1) * P], m.ident[:])
                mm.then_inc(xT_ps, 1)

            def project(b, g):
                n = 4 * b + g
                if g == 0:
                    pe.wait_ge(x1T_s, b + 1)
                pe.wait_ge(q_s, n)
                for h in range(4):
                    for k in range(KT):
                        mm = nc.tensor.matmul(bank(QB, h * P, (h + 1) * P), wqkv[:, k, 0, (4 * g + h) * P:(4 * g + h + 1) * P],
                                              x1T[:, k], start=(k == 0), stop=(k == KT - 1))
                mm.then_inc(q_ps, 1)
                pe.wait_ge(k_s, n)
                for h in range(4):
                    for k in range(KT):
                        mm = nc.tensor.matmul(bank(KB, h * P, (h + 1) * P), wqkv[:, k, 1, (4 * g + h) * P:(4 * g + h + 1) * P],
                                              x1T[:, k], start=(k == 0), stop=(k == KT - 1))
                mm.then_inc(k_ps, 1)
                pe.wait_ge(v_s, n)
                for k in range(KT):
                    mm = nc.tensor.matmul(bank(VB), x1T[:, k], wqkv[:, k, 2, 4 * g * P:(4 * g + 4) * P],
                                          start=(k == 0), stop=(k == KT - 1))
                mm.then_inc(v_ps, 1)

            def scores(b, g):
                n = 4 * b + g
                pe.wait_ge(q_s, n + 1)
                pe.wait_ge(k_s, n + 1)
                for h in range(4):
                    mm = nc.tensor.matmul(bank(SB, h * P, (h + 1) * P), qT[:, h], kT[:, h], start=True, stop=True)
                mm.then_inc(scores_s, 1)

            def turn_p(b, g):
                n = 4 * b + g
                pe.wait_ge(pn_s, n + 1)
                pe.wait_ge(pts_s, n)
                for h in range(4):
                    mm = nc.tensor.transpose(bank(TB, h * P, (h + 1) * P), pn[:, h], m.ident[:])
                mm.then_inc(pt_ps, 1)

            def pv(b, g):
                n = 4 * b + g
                pe.wait_ge(pts_s, n + 1)
                pe.wait_ge(v_s, n + 1)
                pe.wait_ge(oT_s, n)
                for h in range(4):
                    mm = nc.tensor.matmul(bank(OB, h * P, (h + 1) * P), vv[:, g % 2, h * P:(h + 1) * P], pts[:, h],
                                          start=True, stop=True)
                mm.then_inc(pv_s, 1)

            def out_proj(b, g):
                n = 4 * b + g
                pe.wait_ge(oT_s, n + 1)
                if g == 0:
                    pe.wait_ge(ao_s, b)
                for h in range(4):
                    for k in range(KT):
                        mm = nc.tensor.matmul(bank(AB + k, 0, P), wo[:, 4 * g + h, k * P:(k + 1) * P], oT[:, h],
                                              start=(g == 0 and h == 0), stop=(g == 3 and h == 3))
                mm.then_inc(out_ps, 1)

            def turn_back(b):
                pe.wait_ge(ao_s, b + 1)
                for k in range(KT):
                    mm = nc.tensor.transpose(bank(SB, k * P, (k + 1) * P), ao[:, k], m.ident[:])
                mm.then_inc(back_ps, 1)

            pe.wait_ge(m.dma_w[2], 16)
            pe.wait_ge(m.dma_w[3], 48)
            turn_x(0)
            project(0, 0)

            def body(b, first=False, last=False):
                for g in range(4):
                    if g == 3 and not last:
                        pe.wait_ge(x1T_s, b + 2)
                    if g == 2 and not first:
                        pe.wait_ge(x_s, b)
                    scores(b, g)
                    if g < 3:
                        project(b, g + 1)
                    elif not last:
                        project(b + 1, 0)
                    turn_p(b, g)
                    if g == 2 and not last:
                        turn_x(b + 1)
                    if g == 1 and not first:
                        turn_back(b - 1)
                    if g > 0:
                        out_proj(b, g - 1)
                    elif not first:
                        out_proj(b - 1, 3)
                    pv(b, g)

            bodies(pe, body)
            out_proj(B - 1, 3)
            turn_back(B - 1)

        @block.scalar
        def _(act):
            def copy_v(b, g):
                n = 4 * b + g
                act.wait_ge(v_ps, n + 1)
                nc.scalar.activation(vv[:, g % 2], bank(VB), ACT.Copy).then_inc(v_s, 1)

            def exps(b, g):
                n = 4 * b + g
                act.wait_ge(nmax_s, n + 1)
                act.wait_ge(pn_s, n)
                for h in range(4):
                    ins = nc.scalar.activation(prob[:, h], bank(SB, h * P, (h + 1) * P), ACT.Exp, bias=nmax[:, h:h + 1],
                                               accum_out=rsum[:, h:h + 1])
                ins.then_inc(exp_s, 1)

            def copy_pt(b, g):
                n = 4 * b + g
                act.wait_ge(pt_ps, n + 1)
                act.wait_ge(pv_s, n)
                nc.scalar.activation(pts.rearrange("p h t -> p (h t)"), bank(TB), ACT.Copy).then_inc(pts_s, 1)

            copy_v(0, 0)

            def body(b, first=False, last=False):
                for g in range(4):
                    exps(b, g)
                    if g < 3:
                        copy_v(b, g + 1)
                    elif not last:
                        copy_v(b + 1, 0)
                    copy_pt(b, g)

            bodies(act, body)

        @block.vector
        def _(dve):
            dve.wait_ge(b_loaded, 16)
            nc.vector.tensor_scalar(bq[:, 0:H], bq[:, 0:H], SCALE2, None, ALU.mult).then_inc(vstep, 1)
            dve.wait_ge(vstep, 1)

            def stats_x(c):
                nc.vector.bn_stats(stats, row(m.X, c)).then_inc(vstep, 1)
                dve.wait_ge(vstep, 2 * c + 2)
                carry(dve, m)
                nc.vector.bn_aggr(mv, stats).then_inc(vstep, 1)
                dve.wait_ge(vstep, 2 * c + 3)
                nc.vector.tensor_scalar(var, mv[:, 1:2], EPS, None, ALU.add).then_inc(var_s, 1)

            def norm_x(c):
                dve.wait_ge(rstd_s, c + 1)
                nc.vector.tensor_scalar(xn, row(m.X, c), mv[:, 0:1], rstd, ALU.subtract, ALU.mult).then_inc(xn_s, 1)

            def modulate(c):
                dve.wait_ge(xT_ps, c + 1)
                for k in range(KT):
                    ins = nc.vector.tensor_scalar(x1T[:, k], bank(SB, k * P, (k + 1) * P), col(m.ada, KT + k, c),
                                                  col(m.ada, k, c), ALU.mult, ALU.add)
                ins.then_inc(x1T_s, 1)

            def copy_qk(b, g):
                n = 4 * b + g
                dve.wait_ge(q_ps, n + 1)
                nc.vector.scalar_tensor_tensor(out=qT, in0=four(bank(QB)), scalar=SCALE2,
                                               in1=bq[:, 4 * g:4 * g + 4].unsqueeze(2).broadcast_to([P, 4, P]),
                                               op0=ALU.mult, op1=ALU.add).then_inc(q_s, 1)
                dve.wait_ge(k_ps, n + 1)
                nc.vector.tensor_tensor(kT, four(bank(KB)), bq[:, H + 4 * g:H + 4 * g + 4].unsqueeze(2).broadcast_to([P, 4, P]),
                                        ALU.add).then_inc(k_s, 1)

            def maxes(b, g):
                n = 4 * b + g
                dve.wait_ge(scores_s, n + 1)
                nc.vector.tensor_reduce(nmax, four(bank(SB)), AX.X, ALU.max, negate=True).then_inc(nmax_s, 1)

            def recip(b, g):
                n = 4 * b + g
                dve.wait_ge(exp_s, n + 1)
                nc.vector.reciprocal(rinv, rsum).then_inc(rinv_s, 1)

            def copy_o(b, g):
                n = 4 * b + g
                dve.wait_ge(pv_s, n + 1)
                dve.wait_ge(out_ps, n)
                nc.vector.tensor_tensor(oT, four(bank(OB)), bq[:, 2 * H + 4 * g:2 * H + 4 * g + 4].unsqueeze(2).broadcast_to([P, 4, P]),
                                        ALU.add).then_inc(oT_s, 1)

            def gate(b):
                dve.wait_ge(out_ps, 4 * (b + 1))
                for k in range(KT):
                    ins = nc.vector.tensor_scalar(ao[:, k], bank(AB + k, 0, P), col(m.ada, 2 * KT + k, b), col(m.gb, k, b),
                                                  ALU.mult, ALU.add)
                ins.then_inc(ao_s, 1)

            def add(b):
                dve.wait_ge(back_ps, b + 1)
                nc.vector.tensor_tensor(row(m.XA, b), row(m.X, b), bank(SB, 0, D), ALU.add).then_inc(x_s, 1)

            stats_x(0)
            norm_x(0)
            modulate(0)
            copy_qk(0, 0)

            def body(b, first=False, last=False):
                for g in range(4):
                    maxes(b, g)
                    recip(b, g)
                    if g == 0 and not last:
                        stats_x(b + 1)
                    if g == 1 and not last:
                        norm_x(b + 1)
                    if g < 3:
                        copy_qk(b, g + 1)
                    elif not last:
                        copy_qk(b + 1, 0)
                    if g == 2 and not last:
                        modulate(b + 1)
                    if g == 1 and not first:
                        add(b - 1)
                    if g == 0 and not first:
                        gate(b - 1)
                    copy_o(b, g)

            bodies(dve, body)
            gate(B - 1)
            add(B - 1)

        @block.gpsimd
        def _(pool):
            def pow_x(c):
                pool.wait_ge(var_s, c + 1)
                pool.wait_ge(xn_s, c)
                nc.gpsimd.tensor_tensor(rstd, var, m.nhalf[:, 0:1], ALU.pow).then_inc(rstd_s, 1)

            def normalise(b, g):
                n = 4 * b + g
                pool.wait_ge(rinv_s, n + 1)
                pool.wait_ge(pt_ps, n)
                nc.gpsimd.tensor_tensor(pn, prob, rinv.unsqueeze(2).broadcast_to([P, 4, P]), ALU.mult).then_inc(pn_s, 1)

            def both(b):
                pool.wait_ge(x_s, b + 1)
                nc.gpsimd.tensor_tensor(row(m.X, b), row(m.X, b), row(m.XA, b), ALU.add)

            pow_x(0)

            def body(b, first=False, last=False):
                for g in range(4):
                    normalise(b, g)
                    if g == 0 and not last:
                        pow_x(b + 1)
                    if g == 2 and not first:
                        both(b - 1)

            bodies(pool, body)
            both(B - 1)


def phase_ffn(nc, a, m, sem):
    w = Space(m.work)
    GB = 4
    GT = GB * P
    NG = B // GB
    MC = MLP // P
    xn = w.take(GB * D).rearrange("p (b d) -> p b d", b=GB)
    x2T = w.take(KT * GT).rearrange("p (k t) -> p k t", k=KT)
    hT = w.take(MC * GT).rearrange("p (c t) -> p c t", c=MC)
    fo = w.take(KT * GT).rearrange("p (k t) -> p k t", k=KT)
    x3 = w.take(GB * D).rearrange("p (b d) -> p b d", b=GB)
    x3T = w.take(KT * GT).rearrange("p (k t) -> p k t", k=KT)
    stats = m.cols[:, 0:24].rearrange("p (b s) -> p b s", b=GB)
    mv = m.cols[:, 24:32].rearrange("p (b s) -> p b s", b=GB)
    var, rstd = m.cols[:, 32:36], m.cols[:, 36:40]
    b1 = m.cols[:, 48:56]
    bih = m.cols[:, 64:70]
    bhh = m.cols[:, 72:78]
    bg = m.cols[:, 80:86]
    m.bhh_n = m.cols[:, 76:78]
    w1 = m.ring[:, 4096:6144].rearrange("p (k n) -> p k n", k=KT)
    w2 = m.ring[:, 6144:8192].rearrange("p (c n) -> p c n", c=MC)
    gi = m.big[:].rearrange("p (t c b) -> p c b t", c=GATES, b=B)
    names = ("ff_b_loaded ff_var ff_rstd ff_xn ff_xT_ps ff_x2T ff_h_ps ff_h ff_o_ps ff_fo ff_back_ps ff_x3 ff_x3T_ps "
             "ff_x3T ff_gi_ps ff_gi ff_vstep ff_bg ff_x").split()
    (b_loaded, var_s, rstd_s, xn_s, xT_ps, x2T_s, h_ps, h_s, o_ps, fo_s, back_ps, x3_s, x3T_ps, x3T_s, gi_ps, gi_s,
     vstep, bg_s, x_s) = [sem(n) for n in names]
    HB, XB, OB, RB = 0, 2, 4, 6
    bank = lambda k, lo=0, hi=512: m.ps[:, k, lo:hi]

    def bodies(eng, body):
        for g in range(NG):
            body(g, first=g == 0, last=g == NG - 1)

    with nc.Block() as block:
        @block.sync
        def _(sp):
            sp.dma_start(b1, a["col_L2_cond_ffn_b1"]).then_inc(b_loaded, 16)
            sp.dma_start(bih, a["col_L3_cond_b_ih"]).then_inc(b_loaded, 16)
            sp.dma_start(bhh, a["col_L3_cond_b_hh"]).then_inc(b_loaded, 16)

        @block.tensor
        def _(pe):
            def turn_x(g):
                pe.wait_ge(xn_s, g + 1)
                pe.wait_ge(x3T_s, g - 1) if not (type(g) is int and g == 0) else None
                for k in range(KT):
                    for b in range(GB):
                        mm = nc.tensor.transpose(bank(XB + k, b * P, (b + 1) * P), xn[:, b, k * P:(k + 1) * P], m.ident[:])
                mm.then_inc(xT_ps, 1)

            def up(g, c):
                if c == 0:
                    pe.wait_ge(x2T_s, g + 1)
                if c == 0 and not (type(g) is int and g == 0):
                    pe.wait_ge(gi_s, GATES * (g - 1))
                if c >= 2:
                    pe.wait_ge(h_s, MC * g + c - 1)
                for k in range(KT):
                    mm = nc.tensor.matmul(bank(HB + c % 2), w1[:, k, c * P:(c + 1) * P], x2T[:, k], start=(k == 0), stop=(k == KT - 1))
                mm.then_inc(h_ps, 1)

            def down(g):
                pe.wait_ge(fo_s, g)
                for c in range(MC):
                    pe.wait_ge(h_s, MC * g + c + 1)
                    for k in range(KT):
                        mm = nc.tensor.matmul(bank(OB + k), w2[:, c, k * P:(k + 1) * P], hT[:, c], start=(c == 0), stop=(c == MC - 1))
                mm.then_inc(o_ps, 1)

            def turn_back(g):
                pe.wait_ge(fo_s, g + 1)
                pe.wait_ge(x3_s, g)
                for b in range(GB):
                    for k in range(KT):
                        mm = nc.tensor.transpose(bank(RB + b // 2, (b % 2) * D + k * P, (b % 2) * D + (k + 1) * P),
                                                 fo[:, k, b * P:(b + 1) * P], m.ident[:])
                mm.then_inc(back_ps, 1)

            def turn_x3(g, last=False):
                pe.wait_ge(x3_s, g + 1)
                pe.wait_ge(x2T_s, g + 1 if last else g + 2)
                for k in range(KT):
                    for b in range(GB):
                        mm = nc.tensor.transpose(bank(XB + k, b * P, (b + 1) * P), x3[:, b, k * P:(k + 1) * P], m.ident[:])
                mm.then_inc(x3T_ps, 1)

            def gates(g, last=False):
                pe.wait_ge(x3T_s, g + 1)
                pe.wait_ge(h_s, MC * (g + 1) if last else MC * (g + 2))
                for c in range(GATES):
                    if c >= 2:
                        pe.wait_ge(gi_s, GATES * g + c - 1)
                    for k in range(KT):
                        mm = nc.tensor.matmul(bank(HB + c % 2), m.w_ih[:, k, c * P:(c + 1) * P], x3T[:, k], start=(k == 0), stop=(k == KT - 1))
                    mm.then_inc(gi_ps, 1)

            pe.wait_ge(m.dma_w[1], 16)
            turn_x(0)

            def body(g, first=False, last=False):
                for c in range(MC):
                    up(g, c)
                    if c == 3 and not first:
                        turn_back(g - 1)
                if not first:
                    turn_x3(g - 1)
                down(g)
                if not first:
                    gates(g - 1)
                if not last:
                    turn_x(g + 1)

            bodies(pe, body)
            turn_back(NG - 1)
            turn_x3(NG - 1, last=True)
            gates(NG - 1, last=True)

        @block.scalar
        def _(act):
            act.wait_ge(b_loaded, 48)
            act.wait_ge(bg_s, 1)

            def gelus(g):
                for c in range(MC):
                    act.wait_ge(h_ps, MC * g + c + 1)
                    if c == 0:
                        act.wait_ge(o_ps, g)
                    nc.scalar.activation(hT[:, c], bank(HB + c % 2), ACT.Gelu, bias=b1[:, c:c + 1]).then_inc(h_s, 1)

            def copy_x3(g):
                act.wait_ge(x3T_ps, g + 1)
                act.wait_ge(gi_ps, GATES * g)
                for k in range(KT):
                    ins = nc.scalar.activation(x3T[:, k], bank(XB + k), ACT.Copy)
                ins.then_inc(x3T_s, 1)

            def copy_gates(g):
                for c in range(GATES):
                    act.wait_ge(gi_ps, GATES * g + c + 1)
                    nc.scalar.activation(gi[:, c, bass.ds(GB * g, GB), :], bank(HB + c % 2).rearrange("p (b t) -> p b t", b=GB),
                                         ACT.Identity, bias=bg[:, c:c + 1]).then_inc(gi_s, 1)

            def body(g, first=False, last=False):
                gelus(g)
                if not first:
                    copy_x3(g - 1)
                    copy_gates(g - 1)

            bodies(act, body)
            copy_x3(NG - 1)
            copy_gates(NG - 1)

        @block.vector
        def _(dve):
            dve.wait_ge(b_loaded, 48)
            nc.vector.tensor_tensor(bg[:, 0:4], bih[:, 0:4], bhh[:, 0:4], ALU.add)
            nc.vector.tensor_copy(bg[:, 4:6], bih[:, 4:6]).then_inc(bg_s, 1)

            def norm_x(g):
                for b in range(GB):
                    ins = nc.vector.bn_stats(stats[:, b], row(m.XA, GB * g + b))
                ins.then_inc(vstep, 1)
                dve.wait_ge(vstep, 2 * g + 1)
                carry(dve, m)
                for b in range(GB):
                    ins = nc.vector.bn_aggr(mv[:, b], stats[:, b])
                ins.then_inc(vstep, 1)
                dve.wait_ge(vstep, 2 * g + 2)
                nc.vector.tensor_scalar(var, mv[:, :, 1], EPS, None, ALU.add).then_inc(var_s, 1)
                dve.wait_ge(rstd_s, g + 1)
                dve.wait_ge(xT_ps, g)
                for b in range(GB):
                    ins = nc.vector.tensor_scalar(xn[:, b], row(m.XA, GB * g + b), mv[:, b, 0:1], rstd[:, b:b + 1],
                                                  ALU.subtract, ALU.mult)
                ins.then_inc(xn_s, 1)

            def modulate(g):
                dve.wait_ge(xT_ps, g + 1)
                dve.wait_ge(h_ps, MC * g)
                for k in range(KT):
                    for b in range(GB):
                        ins = nc.vector.tensor_scalar(x2T[:, k, b * P:(b + 1) * P], bank(XB + k, b * P, (b + 1) * P),
                                                      col(m.ada, 4 * KT + k, GB * g + b), col(m.ada, 3 * KT + k, GB * g + b),
                                                      ALU.mult, ALU.add)
                ins.then_inc(x2T_s, 1)

            def gate(g):
                dve.wait_ge(o_ps, g + 1)
                dve.wait_ge(back_ps, g)
                for k in range(KT):
                    for b in range(GB):
                        ins = nc.vector.tensor_scalar(fo[:, k, b * P:(b + 1) * P], bank(OB + k, b * P, (b + 1) * P),
                                                      col(m.ada, 5 * KT + k, GB * g + b), col(m.gb, 2 + k, GB * g + b),
                                                      ALU.mult, ALU.add)
                ins.then_inc(fo_s, 1)

            def add(g):
                dve.wait_ge(back_ps, g + 1)
                dve.wait_ge(x3T_ps, g)
                dve.wait_ge(x_s, g)
                for h in range(2):
                    ins = nc.vector.tensor_tensor(x3[:, 2 * h:2 * h + 2], m.X[:, bass.ds(GB * g + 2 * h, 2), :],
                                                  bank(RB + h).rearrange("p (b d) -> p b d", b=2), ALU.add)
                ins.then_inc(x3_s, 1)

            norm_x(0)
            modulate(0)

            def body(g, first=False, last=False):
                if not first:
                    add(g - 1)
                if not last:
                    norm_x(g + 1)
                    modulate(g + 1)
                gate(g)

            bodies(dve, body)
            add(NG - 1)

        @block.gpsimd
        def _(pool):
            def pow_x(g):
                pool.wait_ge(var_s, g + 1)
                pool.wait_ge(xn_s, g)
                nc.gpsimd.tensor_tensor(rstd, var, m.nhalf[:, 0:GB], ALU.pow).then_inc(rstd_s, 1)

            def store(g):
                pool.wait_ge(x3_s, g + 1)
                carry(pool, m)
                nc.gpsimd.tensor_copy(m.X[:, bass.ds(GB * g, GB), :], x3).then_inc(x_s, 1)

            pow_x(0)

            def body(g, first=False, last=False):
                if not first:
                    store(g - 1)
                if not last:
                    pow_x(g + 1)

            bodies(pool, body)
            store(NG - 1)


def phase_gru(nc, a, m, sem, out):
    w = Space(m.work)
    hp = w.take(2 * KT * NPART * B, BF16).rearrange("p (u k n) -> p u k n", u=2, k=KT)
    h = w.take(2 * KT * B).rearrange("p (u k b) -> p u k b", u=2, k=KT)
    rest = w.take(KT * B).rearrange("p (k b) -> p k b", k=KT)
    pre = w.take(GATES * B).rearrange("p (c b) -> p c b", c=GATES)
    act_out = w.take(GATES * B).rearrange("p (c b) -> p c b", c=GATES)
    zh = w.take(KT * B).rearrange("p (k b) -> p k b", k=KT)
    mn = w.take(KT * B).rearrange("p (k b) -> p k b", k=KT)
    rn = w.take(KT * B).rearrange("p (k b) -> p k b", k=KT)
    npre = w.take(KT * B).rearrange("p (k b) -> p k b", k=KT)
    bn = w.take(KT * B).rearrange("p (k b) -> p k b", k=KT)
    hist = w.take(KT * B * N).rearrange("p (k b t) -> p k b t", k=KT, b=B)
    res = w.take(2 * 512).rearrange("p (a n) -> p a n", a=2)
    gi = m.big[:].rearrange("p (t n) -> p t n", t=N)
    names = ("gru_h gru_r_ps gru_n_ps gru_z_ps gru_r_pre gru_z_pre gru_n_sum gru_n_pre gru_bn gru_r gru_z gru_n gru_step gru_state "
             "gru_rest gru_kept gru_turned gru_summed gru_stored0 gru_stored1").split()
    (h_s, r_ps, n_ps, z_ps, r_pre, z_pre, n_sum, n_pre, bn_s, r_s, z_s, n_s, step, state_s, rest_s, kept, turned, summed,
     *stored) = [sem(n) for n in names]
    RB, NB, ZB = 0, 1, 2
    LINKS = 3
    hparts = lambda u, j: hp[:, u].rearrange("p k (a b) -> p k a b", a=NPART)[:, :, j]
    parts_sum = lambda k: m.ps[:, k, 0:96].rearrange("p (c a b) -> p c b a", c=KT, a=NPART)

    def steps(eng, body):
        with eng.Fori(0, N // UNROLL) as i:
            for s in range(UNROLL):
                body(UNROLL * i + s, s % 2)

    with nc.Block() as block:
        @block.tensor
        def _(pe):
            pe.wait_ge(m.split, 1)

            pe.wait_ge(bn_s, 1)

            def time_step(t, u):
                first = lambda k: m.ps[:, k, 0:96].rearrange("p (c a b) -> p c a b", c=KT, a=NPART)[:, :, 0]
                gate = lambda k: gi[:, bass.ds(t, 1), 2 * k * B:2 * (k + 1) * B].rearrange("p o n -> p (o n)")
                for bk, read, add in ((RB, r_pre, gate(0)), (NB, n_sum, bn.rearrange("p c b -> p (c b)")), (ZB, z_pre, gate(1))):
                    pe.wait_ge(read, t + 1)
                    nc.tensor.matmul(first(bk), m.ident[:], add, start=True, stop=False, skip_group_check=True)
                pe.wait_ge(h_s, t + 1)
                for bk, c0, done in ((RB, 0, r_ps), (NB, 4, n_ps), (ZB, 2, z_ps)):
                    for c in range(KT):
                        for k in range(KT):
                            for j in range(NPART):
                                mm = nc.tensor.matmul(m.ps[:, bk, 48 * c:48 * c + 48],
                                                      m.whp[:, j, k, (c0 + c) * P:(c0 + c + 1) * P], hp[:, u, k],
                                                      start=False, stop=(k == KT - 1 and j == NPART - 1), skip_group_check=True)
                    mm.then_inc(done, 1)

            steps(pe, time_step)
            pe.wait_ge(kept, N + 2)
            for q in range(B // 2):
                if q >= 4:
                    pe.wait_ge(summed, q - 3)
                for b in range(2):
                    for k in range(KT):
                        mm = nc.tensor.transpose(m.ps[:, 4 + q % 4, b * D + k * P:b * D + (k + 1) * P], hist[:, k, 2 * q + b],
                                                 m.ident[:])
                mm.then_inc(turned, 1)

        @block.scalar
        def _(act):
            def time_step(t, u):
                act.wait_ge(r_pre, t + 2)
                nc.scalar.activation(act_out[:, 0:2], pre[:, 0:2], ACT.Sigmoid).then_inc(r_s, 1)
                act.wait_ge(z_pre, t + 2)
                nc.scalar.activation(act_out[:, 2:4], pre[:, 2:4], ACT.Sigmoid).then_inc(z_s, 1)
                act.wait_ge(n_pre, t + 1)
                nc.scalar.activation(act_out[:, 4:6], npre, ACT.Tanh).then_inc(n_s, 1)

            steps(act, time_step)

        @block.vector
        def _(dve):
            for s in (r_pre, n_sum, z_pre):
                dve.sem_inc(s, 1)
            nc.vector.tensor_copy(bn, m.bhh_n.unsqueeze(2).broadcast_to([P, KT, B])).then_inc(bn_s, 1)
            c = Chain(dve, step)
            c.link(nc.vector.tensor_copy(h[:, 0], m.condT[:]))
            c.link(nc.vector.tensor_copy(hparts(0, 0), h[:, 0]))
            c.link(nc.vector.tensor_tensor(rest, h[:, 0], hparts(0, 0), ALU.subtract))
            c.link(nc.vector.tensor_copy(hparts(0, 1), rest))
            nc.vector.tensor_tensor(hparts(0, 2), rest, hparts(0, 1), ALU.subtract).then_inc(h_s, 1)
            base = c.n

            def time_step(t, u):
                v = nc.vector
                c = Chain(dve, step, LINKS * t + base)
                dve.wait_ge(r_ps, t + 1)
                v.tensor_reduce(pre[:, 0:2], parts_sum(RB), AX.X, ALU.add).then_inc(r_pre, 1)
                dve.wait_ge(n_ps, t + 1)
                v.tensor_reduce(pre[:, 4:6], parts_sum(NB), AX.X, ALU.add).then_inc(n_sum, 1)
                dve.wait_ge(n_sum, t + 2)
                dve.wait_ge(r_s, t + 1)
                v.tensor_tensor(rn, pre[:, 4:6], act_out[:, 0:2], ALU.mult).then_inc(step, 1)
                dve.wait_ge(z_ps, t + 1)
                v.tensor_reduce(pre[:, 2:4], parts_sum(ZB), AX.X, ALU.add).then_inc(z_pre, 1)
                dve.wait_ge(step, LINKS * t + base + 1)
                v.tensor_tensor(npre, rn, gi[:, bass.ds(t, 1), 4 * B:6 * B].rearrange("p o (c b) -> p (o c) b", b=B),
                                ALU.add).then_inc(n_pre, 1)
                dve.wait_ge(z_s, t + 1)
                v.tensor_tensor(zh, act_out[:, 2:4], h[:, u], ALU.mult).then_inc(step, 1)
                dve.wait_ge(n_s, t + 1)
                v.scalar_tensor_tensor(out=mn, in0=act_out[:, 2:4], scalar=1.0, in1=act_out[:, 4:6],
                                       op0=ALU.subtract, op1=ALU.mult).then_inc(step, 1)
                dve.wait_ge(kept, t + 1)
                dve.wait_ge(step, LINKS * t + base + 3)
                v.tensor_tensor(hparts(1 - u, 0), zh, mn, ALU.subtract)
                v.tensor_tensor(h[:, 1 - u], zh, mn, ALU.subtract).then_inc(state_s, 1)
                dve.wait_ge(state_s, t + 1)
                v.tensor_tensor(rest, h[:, 1 - u], hparts(1 - u, 0), ALU.subtract)
                v.tensor_tensor(hparts(1 - u, 1), h[:, 1 - u], hparts(1 - u, 0), ALU.subtract).then_inc(rest_s, 1)
                dve.wait_ge(rest_s, t + 1)
                v.tensor_tensor(hparts(1 - u, 2), rest, hparts(1 - u, 1), ALU.subtract).then_inc(h_s, 1)

            steps(dve, time_step)
            for q in range(B // 2):
                dve.wait_ge(turned, q + 1)
                if q >= 2:
                    dve.wait_ge(stored[q % 2], 16 * (q // 2))
                nc.vector.tensor_tensor(res[:, q % 2], m.ps[:, 4 + q % 4], m.X[:, 2 * q:2 * q + 2].rearrange("p b d -> p (b d)"),
                                        ALU.add).then_inc(summed, 1)

        @block.gpsimd
        def _(pool):
            pool.sem_inc(kept, 2)

            def time_step(t, u):
                pool.wait_ge(state_s, t + 1)
                carry(pool, m)
                nc.gpsimd.tensor_copy(hist[:, :, :, bass.ds(t, 1)].rearrange("p k b o -> p k (b o)"), h[:, 1 - u]).then_inc(kept, 1)

            steps(pool, time_step)

        @block.sync
        def _(sp):
            for q in range(B // 2):
                sp.wait_ge(summed, q + 1)
                sp.dma_start(out[2 * q:2 * q + 2].rearrange("b t d -> t b d"), res[:, q % 2].rearrange("p (b d) -> p b d", b=2)
                             ).then_inc(stored[q % 2], 16)
            for u in range(2):
                sp.wait_ge(stored[u], 16 * (B // 4))


def kernel(**inputs):
    import numpy as np
    import concourse.bacc as bacc
    from concourse.bass_utils import run_bass_kernel_spmd

    laid = {n: np.ascontiguousarray(v) for n, v in inputs.items()}
    laid["condT"] = np.ascontiguousarray(laid["cond_2048"].T)
    for g in "qkv":
        laid[f"W{g}T"] = np.ascontiguousarray(laid.pop(f"L0_cond_W{g}").T)
    for n in ("L1_cond_b_emb", "L2_cond_ada_b", "L1_cond_g_norm", "L2_cond_qkv_b", "L2_cond_out_b", "L2_cond_ffn_b1",
              "L2_cond_ffn_b2", "L3_cond_b_ih", "L3_cond_b_hh"):
        laid["col_" + n] = np.ascontiguousarray(laid.pop(n).reshape(-1, P).T)
    nc = bacc.Bacc("TRN2", target_bir_lowering=False, num_devices=1)
    args = {n: nc.dram_tensor(f"in_{n}", v.shape, mybir.dt.from_np(v.dtype), kind="ExternalInput").ap()
            for n, v in laid.items()}
    out = nc.dram_tensor("out", (B, N, D), F32, kind="ExternalOutput").ap()
    program(nc, args, out)
    r = run_bass_kernel_spmd(nc, [{f"in_{n}": v for n, v in laid.items()}], core_ids=[0])
    return r.results[0]["out"]
```

```python
from contextlib import ExitStack

import concourse.bass as bass
import numpy as np
from concourse import mybir

ALU = mybir.AluOpType
ACT = mybir.ActivationFunctionType
AX = mybir.AxisListType
F32 = mybir.dt.float32
BF16 = mybir.dt.bfloat16

P = 128
B, N, D = 16, 128, 256
KT = D // P
H = 16
NEG = -1e30
NPART = 3

DH0 = N // H
TERMS = NPART * NPART * DH0
ROWS0 = TERMS + NPART
PAIRS = H // 2

DH1 = D // H
EPS = 1e-6

DH2 = 128
INNER = H * DH2
MLP = 4 * D
SCALE2 = float(DH2) ** -0.5

GATES = 3 * KT
UNROLL = 8
IDLE = 3
SMALL = 8 + 8 + 4


def carry(eng, m):
    eng.sem_inc(m.passed, 1)


class Chain:

    def __init__(self, eng, sem, base=0):
        self.eng, self.sem, self.base, self.n = eng, sem, base, 0

    def link(self, ins):
        self.n += 1
        ins.then_inc(self.sem, 1)
        self.eng.wait_ge(self.sem, self.base + self.n)


def program(nc, a, out):
    with ExitStack() as ctx:
        def sb(name, shape, dt=F32):
            return ctx.enter_context(nc.sbuf_tensor(name, shape, dt))

        def sem(name):
            return ctx.enter_context(nc.semaphore(name))

        m = Mem()
        m.ps = ctx.enter_context(nc.psum_tensor("ps", [P, 8, 512], F32))
        m.X = sb("X", [P, B, D])
        m.ident = sb("ident", [P, P])
        m.identb = sb("identb", [P, P], BF16)
        m.condT = sb("condT", [P, KT, B])
        m.mod1 = sb("mod1", [P, 2 * KT, B])
        m.ada = sb("ada", [P, 6 * KT, B])
        m.A1 = sb("A1", [P, KT, B])
        m.gb = sb("gb", [P, 2 * KT, B])
        m.nhalf = sb("nhalf", [P, 2 * H])
        m.w_qkv1 = sb("w_qkv1", [P, KT, 3 * D])
        m.w_out1 = sb("w_out1", [P, KT, D])
        m.w_ih = sb("w_ih", [P, KT, 3 * D])
        m.whp = sb("whp", [P, NPART, KT, 3 * D], BF16)
        m.big = sb("big", [P, KT * 3 * INNER])
        m.ring = sb("ring", [P, 8192])
        m.work = sb("work", [P, 13824])
        m.XA = m.work[:, 9728:13824].rearrange("p (b d) -> p b d", b=B)
        m.cols = sb("cols", [P, 512])
        m.ssq = m.cols[:, 480:480 + B]
        m.gq, m.gk = m.cols[:, 208:209], m.cols[:, 209:210]
        m.bq, m.b1 = m.cols[:, 288:336], m.cols[:, 336:344]
        m.bih, m.bhh = m.cols[:, 344:350], m.cols[:, 352:358]
        m.small_loaded = sem("small_loaded")
        m.passed = sem("passed")
        m.dma_x = sem("x_loaded")
        m.dma_w = [sem(f"w_loaded{k}") for k in range(4)]
        setup(nc, a, m, sem)
        phase_l0(nc, a, m, sem)
        phase_l1(nc, a, m, sem)
        phase_l2(nc, a, m, sem)
        phase_ffn(nc, a, m, sem)
        phase_gru(nc, a, m, sem, out)


class Mem:
    pass


def load_l2(sp, a, m):
    sp.dma_start(m.big[:].rearrange("p (k n) -> p k n", k=KT),
                 a["L2_cond_qkv_w"].rearrange("(k p) n -> p k n", p=P)).then_inc(m.dma_w[2], 16)
    for n, c0, c1, k in (("L2_cond_out_w", 0, 4096, H), ("L2_cond_ffn_w1", 4096, 6144, KT), ("L2_cond_ffn_w2", 6144, 8192, 8)):
        sp.dma_start(m.ring[:, c0:c1].rearrange("p (k n) -> p k n", k=k),
                     a[n].rearrange("(k p) n -> p k n", p=P)).then_inc(m.dma_w[3], 16)


def setup(nc, a, m, sem):
    m.cond_loaded, m.cond_ps, m.cond_step = sem("cond_loaded"), sem("cond_ps"), sem("cond_step")
    stacks = m.big[:].rearrange("p (s n) -> p s n", s=3)
    m.vz0 = m.work[:, 13824 - 2 * 2 * H * 32:].rearrange("p (u k h c) -> p u k h c", u=2, k=2, h=H)
    vstep, gstep = sem("setup_vstep"), sem("setup_gstep")
    ones = np.array([0x3F803F80], np.uint32).view(np.float32).item()
    with nc.Block() as block:
        @block.gpsimd
        def _(pool):
            c = Chain(pool, gstep)
            c.link(nc.gpsimd.memset(m.ident[:], 0.0))
            c.link(nc.gpsimd.memset(m.identb[:], 0.0))
            c.link(nc.gpsimd.memset(m.nhalf[:], -0.5))
            for t in (m.ident, m.identb):
                c.link(nc.gpsimd.affine_select(out=t[:], in_=t[:], compare_op=ALU.not_equal, fill=1.0, base=0,
                                               pattern=[[-1, P]], channel_multiplier=1))
            nc.gpsimd.memset(stacks[64:96, 0, 0:4096], ones)

        @block.vector
        def _(dve):
            nc.vector.memset(m.vz0, 0.0).then_inc(vstep, 1)
            nc.vector.memset(stacks[64:96, 1, 0:4096], ones)
            dve.wait_ge(vstep, 1)
            blocks = m.vz0.rearrange("p u k (g r j) c -> p (u k g) r j c", r=2, j=4)
            for r in range(2):
                nc.vector.memset(blocks[:, :, r, :, 16 * r + 8:16 * r + 16], 1.0)


def cond_views(m):
    w_emb = m.ring[:, 0:1024].rearrange("p (k n) -> p k n", k=KT)
    ada_w = m.ring[:, 1024:4096].rearrange("p (k n) -> p k n", k=KT)
    at, views = 400, []
    for n in (4, 12, 2, 2, 2):
        views.append(m.cols[:, at:at + n])
        at += n
    return w_emb, ada_w, views


def cond_load(sp, a, m):
    w_emb, ada_w, (b_emb, ada_b, g_norm, out_b, ffn_b2) = cond_views(m)
    for k, v in ((a["L1_cond_W_emb"], w_emb), (a["L2_cond_ada_w"], ada_w)):
        sp.dma_start(v, k.rearrange("(k p) n -> p k n", p=P)).then_inc(m.cond_loaded, 16)
    sp.dma_start(m.condT[:], a["condT"].rearrange("(k p) b -> p k b", p=P)).then_inc(m.cond_loaded, 16)
    for src, dst in (("L1_cond_b_emb", b_emb), ("L2_cond_ada_b", ada_b), ("L1_cond_g_norm", g_norm),
                     ("L2_cond_out_b", out_b), ("L2_cond_ffn_b2", ffn_b2)):
        sp.dma_start(dst, a["col_" + src]).then_inc(m.cond_loaded, 16)


def cond_products(nc, pe, m, bank):
    w_emb, ada_w, _ = cond_views(m)
    pe.wait_ge(m.cond_loaded, 16 * 8)
    for w, n, c0 in ((w_emb, 4, 0), (ada_w, 12, 4)):
        for c in range(n):
            for k in range(KT):
                mm = nc.tensor.matmul(m.ps[:, bank, (c0 + c) * B:(c0 + c + 1) * B], w[:, k, c * P:(c + 1) * P],
                                      m.condT[:, k, :], start=(k == 0), stop=(k == KT - 1))
    mm.then_inc(m.cond_ps, 1)


def cond_vectors(nc, dve, m, bank):
    _, _, (b_emb, ada_b, g_norm, out_b, ffn_b2) = cond_views(m)
    tmp = m.cols[:, 432:464].rearrange("p (k b) -> p k b", k=KT)
    bc = lambda v: v.unsqueeze(2).broadcast_to([P, v.shape[1], B])
    c = Chain(dve, m.cond_step)
    dve.wait_ge(m.cond_ps, 1)
    dve.wait_ge(m.cond_loaded, 16 * 8)
    mp = m.ps[:, bank, 0:256].rearrange("p (c b) -> p c b", b=B)
    c.link(nc.vector.tensor_tensor(m.mod1[:], mp[:, 0:4], bc(b_emb), ALU.add))
    c.link(nc.vector.tensor_tensor(m.ada[:], mp[:, 4:16], bc(ada_b), ALU.add))
    c.link(nc.vector.tensor_scalar(tmp, m.mod1[:, 0:2], 1.0, None, ALU.add))
    c.link(nc.vector.tensor_tensor(m.A1[:], tmp, bc(g_norm), ALU.mult))
    for g in (1, 4):
        s = m.ada[:, g * KT:(g + 1) * KT]
        c.link(nc.vector.tensor_scalar(s, s, 1.0, None, ALU.add))
    c.link(nc.vector.tensor_tensor(m.gb[:, 0:2], m.ada[:, 4:6], bc(out_b), ALU.mult))
    c.link(nc.vector.tensor_tensor(m.gb[:, 2:4], m.ada[:, 10:12], bc(ffn_b2), ALU.mult))


def load_stream(sp, a, m):
    for q in range(4):
        s = slice(4 * q, 4 * q + 4)
        sp.dma_start(m.X[:, s, :], a["x"][s].rearrange("b n d -> n b d")).then_inc(m.dma_x, 16)


def load_l1(sp, a, m):
    sp.dma_start(m.w_qkv1[:], a["L1_cond_W_qkv"].rearrange("(k p) n -> p k n", p=P)).then_inc(m.dma_w[0], 16)
    sp.dma_start(m.w_out1[:], a["L1_cond_W_out"].rearrange("(k p) n -> p k n", p=P)).then_inc(m.dma_w[0], 16)
    sp.dma_start(m.w_ih[:], a["L3_cond_W_ih"].rearrange("(k p) n -> p k n", p=P)).then_inc(m.dma_w[1], 16)
    for g in range(8):
        r = slice(DH1 * g, DH1 * (g + 1))
        sp.dma_start(m.gq[r, :], a["L1_cond_g_q"].unsqueeze(1)).then_inc(m.small_loaded, 16)
        sp.dma_start(m.gk[r, :], a["L1_cond_g_k"].unsqueeze(1)).then_inc(m.small_loaded, 16)
    for n, dst in (("L2_cond_qkv_b", m.bq), ("L2_cond_ffn_b1", m.b1), ("L3_cond_b_ih", m.bih), ("L3_cond_b_hh", m.bhh)):
        sp.dma_start(dst, a["col_" + n]).then_inc(m.small_loaded, 16)


def phase_l0(nc, a, m, sem):
    stacks = m.big[:].rearrange("p (s n) -> p s n", s=3)
    q_st = stacks[:, 0, 0:4096].bitcast(BF16).rearrange("p (u h t) -> p u h t", u=2, h=H)
    k_st = stacks[:, 1, 0:4096].bitcast(BF16).rearrange("p (u h t) -> p u h t", u=2, h=H)
    w = Space(m.work)
    xs = w.take(2 * D).rearrange("p (u t) -> p u t", u=2)
    mask = w.take(2 * D).rearrange("p (u t) -> p u t", u=2)
    w3 = w.take(3 * P).rearrange("p (g o) -> p g o", g=3)
    qk = w.take(2 * D)
    rest = w.take(2 * D)
    parts = w.take(NPART * 2 * D, BF16).rearrange("p (a n) -> p a n", a=NPART)
    vz = m.vz0
    prob = w.take(4 * 4 * D).rearrange("p (a s k t) -> p a s k t", a=4, s=2, k=2)
    yraw = w.take(2 * D)
    rinv = w.take(D)
    yn = w.take(D)
    sqx = w.take(D)
    bias32 = w.take(D)
    bias_r = w.take(D)
    bparts = w.take(NPART * D, BF16).rearrange("p (a n) -> p a n", a=NPART)
    sel = w.take(4 * P).rearrange("p (e g c) -> p e g c", e=2, g=2)
    mrow = w.take(2 * P, BF16).rearrange("p (f t) -> p f t", f=2)
    MC = 2 * H // 2
    mparts = w.take(2 * NPART * MC, BF16).rearrange("p (f a c) -> p f a c", f=2, a=NPART)
    nmax = m.cols[:, 0:2 * MC].rearrange("p (f c) -> p f c", f=2)
    mrest = m.cols[:, 48:48 + MC]
    b0 = m.cols[:, 128:129]
    scratch = nc.dram_tensor("qk_scratch", [2, 2, NPART, DH0, H, D], BF16, kind="Internal").ap()
    bias_d = nc.dram_tensor("bias_scratch", [B, NPART, D], BF16, kind="Internal").ap()
    names = ("l0_w_loaded l0_bias_split l0_bias_stored l0_qk_proj l0_qk_evac l0_v_proj l0_v_evac "
             "l0_parts_ready l0_scr_written l0_by_query l0_nmax l0_mstep l0_mparts l0_mturned l0_mrow l0_by_key l0_exp "
             "l0_pv l0_yraw l0_selected l0_rinv l0_normed l0_x1 l0_gstep l0_ones l0_b_loaded l0_vstep l0_squared l0_pstep").split()
    (w_loaded, bias_split, bias_stored, qk_proj, qk_evac, v_proj, v_evac, parts_ready, scr_written,
     by_query, nmax_s, mstep, mparts_s, mturned, mrow_s, by_key, exp_s, pv_s, yraw_s, selected, rinv_s, normed,
     x1_s, gstep, ones_s, b_loaded, vstep, squared, pstep) = [sem(n) for n in names]
    xs_loaded = [sem(f"l0_xs_loaded{u}") for u in range(2)]
    stack_loaded = [sem(f"l0_stack_loaded{f}") for f in range(2)]
    max_loaded = [sem(f"l0_max_loaded{f}") for f in range(2)]
    SCALE0 = float(DH0) ** -0.5
    LOADS = 16 * (NPART + 2)
    ROWSB = ROWS0 + NPART
    A_BANK, S_BANK, Y_BANK, J_BANK = 0, 2, 6, 7
    exists = lambda c: not (type(c) is int and c >= B)
    before = lambda c: type(c) is int and c < 0

    def bodies(eng, body):
        body(0)
        with eng.Fori(1, B // 2 - 2) as i:
            body(i)
        body(B // 2 - 2)
        body(B // 2 - 1)

    with nc.Block() as block:
        @block.sync
        def _(sp):
            def load_x(c, u):
                sp.dma_start(xs[:, u], a["x"][bass.ds(c, 1)].rearrange("o c t -> c (o t)")).then_inc(xs_loaded[u], 16)
                sp.dma_start(mask[:, u], a["cond_2048"][bass.ds(c, 1)].broadcast_to([P, D])).then_inc(xs_loaded[u], 16)

            def store_parts(c, u):
                sp.wait_ge(parts_ready, c + 1)
                carry(sp, m)
                for g in range(2):
                    sp.dma_start(scratch[u, g].rearrange("a d h t -> (d h) a t"),
                                 parts[:, :, g * D:(g + 1) * D]).then_inc(scr_written, 16)
                sp.wait_ge(scr_written, 32 * (c + 1))
                carry(sp, m)

            def load_stack(c, u, f):
                hs = slice(8 * f, 8 * f + 8)
                flat = lambda t: t.rearrange("p h t -> p (h t)")
                for i in range(NPART):
                    sp.dma_start(flat(q_st[3 * DH0 * i:3 * DH0 * (i + 1), u, hs]),
                                 scratch[u, 0, i, :, hs].rearrange("d h t -> d (h t)").unsqueeze(0).broadcast_to([NPART, DH0, 8 * D])
                                 ).then_inc(stack_loaded[f], 16)
                src_k = scratch[u, 1, :, :, hs].rearrange("a d h t -> (a d) (h t)")
                sp.dma_start(flat(k_st[0:TERMS, u, hs]), src_k.unsqueeze(0).broadcast_to([NPART, NPART * DH0, 8 * D])
                             ).then_inc(stack_loaded[f], 16)
                sp.dma_start(k_st[TERMS:ROWS0, u, hs],
                             bias_d[bass.ds(c, 1)].rearrange("o a t -> (o a) t").unsqueeze(1).broadcast_to([NPART, 8, D])
                             ).then_inc(stack_loaded[f], 16)

            load_x(0, 0)
            for g, n in enumerate(("WqT", "WkT", "WvT")):
                sp.dma_start(w3[:, g], a[n]).then_inc(w_loaded, 16)
            sp.dma_start(bias32[0:B, :], a["cond_2048"]).then_inc(b_loaded, 16)
            sp.dma_start(b0[0:B, :], a["L0_cond_b"].unsqueeze(0).broadcast_to([B, 1])).then_inc(b_loaded, 16)
            load_x(1, 1)
            cond_load(sp, a, m)
            sp.wait_ge(bias_split, 1)
            sp.dma_start(bias_d, bparts[0:B]).then_inc(bias_stored, 16)
            sp.wait_ge(bias_stored, 16)
            sp.wait_ge(v_proj, 1)
            load_x(2, 0)
            store_parts(0, 0)
            load_stack(0, 0, 0)
            load_stack(0, 0, 1)
            load_stream(sp, a, m)
            store_parts(1, 1)
            for f in range(2):
                sp.wait_ge(stack_loaded[f], LOADS)
                load_stack(1, 1, f)
            for f in range(2):
                sp.wait_ge(stack_loaded[f], 2 * LOADS)
            load_l1(sp, a, m)

            def body(i):
                for u in range(2):
                    b = 2 * i + u
                    if exists(b + 2):
                        store_parts(b + 2, u)
                    for f in range(2):
                        if exists(b + 2):
                            sp.wait_ge(by_key, PAIRS * b + 4 * f + 4)
                            carry(sp, m)
                            load_stack(b + 2, u, f)
                        if f == 0 and exists(b + 3):
                            sp.wait_ge(v_proj, b + 2)
                            carry(sp, m)
                            load_x(b + 3, 1 - u)

            bodies(sp, body)
            sp.wait_ge(by_key, PAIRS * B)
            load_l2(sp, a, m)

        @block.tensor
        def _(pe):
            def proj_qk(c, u, k):
                pe.wait_ge(xs_loaded[u], 32 * (k + 1))
                if type(c) is int and c < 2:
                    if c:
                        pe.wait_ge(v_evac, 1)
                elif type(c) is int and c == 2:
                    pe.wait_ge(qk_evac, 2)
                else:
                    pe.wait_ge(mrow_s, 2 * (c - 2) + 1)
                for g in range(2):
                    mm = nc.tensor.matmul(m.ps[:, J_BANK, g * D:(g + 1) * D], w3[:, g], xs[:, u], start=True, stop=True)
                mm.then_inc(qk_proj, 1)

            def proj_v(c, u):
                if type(c) is int and c < 2:
                    pe.wait_ge(qk_evac, 1)
                    if c == 1:
                        pe.wait_ge(mrow_s, 2)
                else:
                    pe.wait_ge(normed, c - 1)
                for k in range(2):
                    mm = nc.tensor.matmul(m.ps[:, J_BANK, k * P:(k + 1) * P], xs[:, u, k * P:(k + 1) * P], w3[:, 2],
                                          start=True, stop=True)
                mm.then_inc(v_proj, 1)

            def scores_by_query(c, u, n):
                if n % 8 == 0:
                    pe.wait_ge(stack_loaded[n // 8], LOADS * (c + 1))
                if not (type(c) is int and c == 0 and n < 2):
                    pe.wait_ge(nmax_s, H * c + n - 1)
                for q in range(2):
                    mm = nc.tensor.matmul(m.ps[:, A_BANK + n % 2, q * D:(q + 1) * D], q_st[0:ROWS0, u, n, q * P:(q + 1) * P],
                                          k_st[0:ROWS0, u, n], start=True, stop=True)
                mm.then_inc(by_query, 1)

            def turn_max(c, f):
                pe.wait_ge(mparts_s, 2 * c + f + 1)
                if f == 1:
                    pe.wait_ge(qk_evac, B if not exists(c + 3) else c + 3)
                elif not (type(c) is int and c == 0):
                    pe.wait_ge(v_evac, c + 1)
                mm = nc.tensor.matmul(m.ps[0:NPART * MC, J_BANK, 0:P], mparts[:, f].rearrange("p a c -> p (a c)"), m.identb[:],
                                      start=True, stop=True)
                mm.then_inc(mturned, 1)

            def scores_by_key(c, u, p):
                if p % 4 == 0:
                    pe.wait_ge(max_loaded[p // 4], 16 * (c + 1))
                if not (type(c) is int and c == 0 and p < 2):
                    pe.wait_ge(exp_s, PAIRS * c + p - 1)
                for s in range(2):
                    for k in range(2):
                        mm = nc.tensor.matmul(m.ps[:, S_BANK + 2 * (p % 2) + s, k * D:(k + 1) * D],
                                              k_st[0:ROWSB, u, 2 * p + s, k * P:(k + 1) * P], q_st[0:ROWSB, u, 2 * p + s],
                                              start=True, stop=True)
                mm.then_inc(by_key, 1)

            def pv(c, u, g, k):
                if g == 0 and k == 0:
                    pe.wait_ge(v_evac, c + 1)
                    if not (type(c) is int and c == 0):
                        pe.wait_ge(yraw_s, c)
                pe.wait_ge(exp_s, PAIRS * c + 2 * g + 2)
                for j in range(4):
                    mm = nc.tensor.matmul(m.ps[32 * j:32 * j + 32, Y_BANK, (g // 2) * D:(g // 2 + 1) * D],
                                          vz[:, u, k, 4 * g + j], prob[:, 2 * (g % 2) + j // 2, j % 2, k],
                                          start=(g % 2 == 0 and k == 0), stop=(g % 2 == 1 and k == 1),
                                          tile_position=(0, 32 * j))
                if k == 1:
                    mm.then_inc(pv_s, 1)

            def select(c):
                pe.wait_ge(yraw_s, c + 1)
                if type(c) is int and c == 0:
                    pe.wait_ge(ones_s, 1)
                pe.wait_ge(mrow_s, min(2 * c + 4, 2 * B) if type(c) is int else 2 * c + 4)
                for e in range(2):
                    for g in range(2):
                        mm = nc.tensor.matmul(m.ps[:, J_BANK, e * D:(e + 1) * D], sel[:, e, g], yraw[:, g * D:(g + 1) * D],
                                              start=(g == 0), stop=(g == 1))
                mm.then_inc(selected, 1)

            pe.wait_ge(w_loaded, 48)
            proj_qk(0, 0, 0)
            proj_v(0, 0)
            proj_qk(1, 1, 0)
            proj_qk(2, 0, 1)
            cond_products(nc, pe, m, Y_BANK)
            for n in range(H):
                scores_by_query(0, 0, n)
                if n == 9:
                    pe.wait_ge(qk_evac, 3)
                    turn_max(0, 0)
            scores_by_key(0, 0, 0)

            def body(i):
                for u in range(2):
                    b = 2 * i + u
                    for p in range(PAIRS):
                        if p < PAIRS - 1:
                            scores_by_key(b, u, p + 1)
                        if exists(b + 1):
                            scores_by_query(b + 1, 1 - u, 2 * p)
                        if p == 5 and exists(b + 1):
                            turn_max(b + 1, 0)
                        if p < 2 and not before(b - 1):
                            pv(b - 1, 1 - u, 3, p)
                        if p >= 2:
                            pv(b, u, p // 2 - 1, p % 2)
                        if exists(b + 1):
                            scores_by_query(b + 1, 1 - u, 2 * p + 1)
                        if p == PAIRS - 1 and exists(b + 1):
                            scores_by_key(b + 1, 1 - u, 0)
                        if p == 1:
                            turn_max(b, 1)
                        if p == 2 and not before(b - 1):
                            select(b - 1)
                        if p == 3 and exists(b + 1):
                            proj_v(b + 1, 1 - u)
                        if p == 6 and exists(b + 3):
                            proj_qk(b + 3, 1 - u, i + (u + 3) // 2)

            bodies(pe, body)
            pv(B - 1, 1, 3, 0)
            pv(B - 1, 1, 3, 1)
            select(B - 1)

        @block.scalar
        def _(act):
            def exps(c, p):
                act.wait_ge(by_key, PAIRS * c + p + 1)
                if not (type(c) is int and c == 0 and p < 4):
                    act.wait_ge(pv_s, 4 * c + p // 2 - 1)
                s = S_BANK + 2 * (p % 2)
                nc.scalar.activation(prob[:, p % 4].rearrange("p s k t -> p s (k t)"), m.ps[:, s:s + 2], ACT.Exp).then_inc(exp_s, 1)

            def copy_max(c, f):
                act.wait_ge(mturned, 2 * c + f + 1)
                if not (type(c) is int and c == 0):
                    act.wait_ge(max_loaded[f], 16 * c)
                nc.scalar.activation(mrow[0:NPART * MC, f], m.ps[0:NPART * MC, J_BANK, 0:P], ACT.Copy).then_inc(mrow_s, 1)

            def load_max(c, u, f):
                act.wait_ge(mrow_s, 2 * c + f + 1)
                carry(act, m)
                act.dma_start(q_st[ROWS0:ROWSB, u, 8 * f:8 * f + 8].rearrange("p h (q t) -> p (h q) t", q=2),
                              mrow[0:NPART * MC, f]).then_inc(max_loaded[f], 16)

            def copy_y(c):
                act.wait_ge(pv_s, 4 * c + 4)
                if not (type(c) is int and c == 0):
                    act.wait_ge(selected, c)
                nc.scalar.activation(yraw, m.ps[:, Y_BANK], ACT.Copy).then_inc(yraw_s, 1)

            def square(c):
                act.wait_ge(x1_s, c + 1)
                if not (type(c) is int and c == 0):
                    act.wait_ge(squared, c)
                nc.scalar.activation(sqx, row(m.X, c), ACT.Square, accum_out=m.ssq[:, bass.ds(c, 1)]).then_inc(squared, 1)

            nc.scalar.activation(sqx[:, 0:1], m.nhalf[:, 0:1], ACT.Exp)
            copy_max(0, 0)
            load_max(0, 0, 0)

            def body(i):
                for u in range(2):
                    b = 2 * i + u
                    for p in range(PAIRS):
                        exps(b, p)
                        if p == 1 and not before(b - 1):
                            copy_y(b - 1)
                        if p == 1:
                            copy_max(b, 1)
                            load_max(b, u, 1)
                        if p == 5 and exists(b + 1):
                            copy_max(b + 1, 0)
                            load_max(b + 1, 1 - u, 0)
                        if p == 6 and not before(b - 1):
                            square(b - 1)

            bodies(act, body)
            copy_y(B - 1)
            square(B - 1)

        @block.vector
        def _(dve):
            c = Chain(dve, gstep)
            nc.vector.memset(sel, 0.0).then_inc(vstep, 1)
            dve.wait_ge(b_loaded, 32)
            c.link(nc.vector.tensor_scalar(bias_r[0:B], bias32[0:B], -NEG, NEG, ALU.mult, ALU.add))
            c.link(nc.vector.tensor_scalar(bias32[0:B], bias32[0:B], b0[0:B], None, ALU.mult))
            c.link(nc.vector.tensor_tensor(bias32[0:B], bias32[0:B], bias_r[0:B], ALU.add))
            c.link(nc.vector.tensor_copy(bparts[0:B, 0], bias32[0:B]))
            c.link(nc.vector.tensor_tensor(bias_r[0:B], bias32[0:B], bparts[0:B, 0], ALU.subtract))
            c.link(nc.vector.tensor_copy(bparts[0:B, 1], bias_r[0:B]))
            nc.vector.tensor_tensor(bparts[0:B, 2], bias_r[0:B], bparts[0:B, 1], ALU.subtract).then_inc(bias_split, 1)
            dve.wait_ge(vstep, 1)
            for e in range(2):
                for g in range(2):
                    ins = nc.vector.tensor_copy(sel[:, e, g, 64 * g:64 * g + 64].rearrange("p (r j d) -> p r j d", r=2, j=4),
                                          m.ident[:].rearrange("p (j r e d) -> p r j e d", j=4, r=2, e=2)[:, :, :, e])
            ins.then_inc(ones_s, 1)

            def evac_qk(c, u):
                dve.wait_ge(qk_proj, c + 1)
                if not (type(c) is int and c == 0):
                    dve.wait_ge(parts_ready, c)
                nc.vector.tensor_copy(qk[:, 0:D], m.ps[:, J_BANK, 0:D])
                nc.vector.scalar_tensor_tensor(out=qk[:, D:2 * D], in0=m.ps[:, J_BANK, D:2 * D], scalar=SCALE0,
                                               in1=mask[:, u], op0=ALU.mult, op1=ALU.mult).then_inc(qk_evac, 1)

            def evac_v(c, u):
                dve.wait_ge(v_proj, c + 1)
                if not (type(c) is int and c < 2):
                    dve.wait_ge(pv_s, 4 * (c - 1))
                dst = vz[:, u].rearrange("p k (g r j) c -> p (k g) r j c", r=2, j=4)
                src = m.ps[:, J_BANK, 0:D].rearrange("p (a r j d) -> p a r j d", a=4, r=2, j=4)
                for r in range(2):
                    ins = nc.vector.tensor_copy(dst[:, :, r, :, 16 * r:16 * r + 8], src[:, :, r])
                ins.then_inc(v_evac, 1)

            def maxes(c, n):
                dve.wait_ge(by_query, H * c + n + 1)
                nc.vector.tensor_reduce(nmax[:, n // 8, 2 * (n % 8):2 * (n % 8) + 2],
                                        m.ps[:, A_BANK + n % 2].rearrange("p (q t) -> p q t", q=2), AX.X, ALU.max,
                                        negate=True).then_inc(nmax_s, 1)

            def split_max(c, f, k):
                s = 2 * (2 * c + f)
                if k == 0:
                    if not (type(c) is int and c == 0):
                        dve.wait_ge(mturned, 2 * c + f - 1)
                    dve.wait_ge(nmax_s, H * c + 8 * f + 8)
                    carry(dve, m)
                    nc.vector.tensor_copy(mparts[:, f, 0], nmax[:, f]).then_inc(mstep, 1)
                elif k == 1:
                    dve.wait_ge(mstep, s + 1)
                    nc.vector.tensor_tensor(mrest, nmax[:, f], mparts[:, f, 0], ALU.subtract)
                    nc.vector.tensor_tensor(mparts[:, f, 1], nmax[:, f], mparts[:, f, 0], ALU.subtract).then_inc(mstep, 1)
                else:
                    dve.wait_ge(mstep, s + 2)
                    nc.vector.tensor_tensor(mparts[:, f, 2], mrest, mparts[:, f, 1], ALU.subtract).then_inc(mparts_s, 1)

            def recip(c):
                dve.wait_ge(selected, c + 1)
                nc.vector.reciprocal(rinv, m.ps[:, J_BANK, D:2 * D]).then_inc(rinv_s, 1)

            def norm(c):
                dve.wait_ge(rinv_s, c + 1)
                if not (type(c) is int and c == 0):
                    dve.wait_ge(x1_s, c)
                nc.vector.tensor_tensor(yn, m.ps[:, J_BANK, 0:D], rinv, ALU.mult).then_inc(normed, 1)

            evac_qk(0, 0)
            evac_v(0, 0)
            evac_qk(1, 1)
            evac_qk(2, 0)
            cond_vectors(nc, dve, m, Y_BANK)
            for n in range(H):
                maxes(0, n)
                if n in (7, 8, 9):
                    split_max(0, 0, n - 7)

            def body(i):
                for u in range(2):
                    b = 2 * i + u
                    for p in range(PAIRS):
                        for s in range(2):
                            n = 2 * p + s
                            if n < 3:
                                split_max(b, 1, n)
                            if exists(b + 1):
                                maxes(b + 1, n)
                                if n in (7, 8, 9):
                                    split_max(b + 1, 0, n - 7)
                            if n == 5 and not before(b - 1):
                                recip(b - 1)
                            if n == 6 and not before(b - 1):
                                norm(b - 1)
                            if n == 8 and exists(b + 1):
                                evac_v(b + 1, 1 - u)
                            if n == 13 and exists(b + 3):
                                evac_qk(b + 3, 1 - u)

            bodies(dve, body)
            recip(B - 1)
            norm(B - 1)

        @block.gpsimd
        def _(pool):
            def split(b):
                c = Chain(pool, pstep, 3 * b)
                pool.wait_ge(qk_evac, b + 1)
                if not (type(b) is int and b == 0):
                    pool.wait_ge(scr_written, 32 * b)
                carry(pool, m)
                c.link(nc.gpsimd.tensor_copy(parts[:, 0], qk))
                c.link(nc.gpsimd.tensor_tensor(rest, qk, parts[:, 0], ALU.subtract))
                carry(pool, m)
                c.link(nc.gpsimd.tensor_copy(parts[:, 1], rest))
                nc.gpsimd.tensor_tensor(parts[:, 2], rest, parts[:, 1], ALU.subtract).then_inc(parts_ready, 1)

            def add(b):
                pool.wait_ge(normed, b + 1)
                nc.gpsimd.tensor_tensor(row(m.X, b), row(m.X, b), yn, ALU.add).then_inc(x1_s, 1)

            for c in range(3):
                split(c)
            pool.wait_ge(m.dma_x, 64)

            def body(i):
                for u in range(2):
                    b = 2 * i + u
                    if not before(b - 1):
                        add(b - 1)
                    if exists(b + 3):
                        split(b + 3)

            bodies(pool, body)
            add(B - 1)


class Space:

    def __init__(self, tile):
        self.tile, self.at = tile, 0

    def take(self, n, dt=F32):
        words = n if dt == F32 else n // 2
        v = self.tile[:, self.at:self.at + words]
        self.at += words
        return v if dt == F32 else v.bitcast(dt)


def row(t, b):
    return t[:, bass.ds(b, 1), :].rearrange("p o n -> p (o n)")


def col(t, c, b):
    return t[:, c, bass.ds(b, 1)]


def phase_l1(nc, a, m, sem):
    w = Space(m.work)
    xn = w.take(D)
    xnT = w.take(2 * KT * P).rearrange("p (u k t) -> p u k t", u=2, k=KT)
    sq = w.take(2 * D)
    qkn = w.take(2 * D)
    qT = w.take(2 * 2 * P).rearrange("p (u g t) -> p u g t", u=2, g=2)
    kz = w.take(2 * 8 * P * 2).rearrange("p (g h t) -> p g h t", g=2, h=8)[:, :, :, :]
    kz = kz.rearrange("p g h (u t) -> p u g h t", u=2)
    vz = w.take(2 * 8 * 64).rearrange("p (u j c) -> p u j c", u=2, j=8)
    prob = w.take(2 * 512).rearrange("p (a n) -> p a n", a=2)
    pts = w.take(2 * 512).rearrange("p (a n) -> p a n", a=2)
    rrep = w.take(D)
    rts = w.take(D)
    oraw = w.take(D)
    oT = w.take(D).rearrange("p (g t) -> p g t", g=2)
    raw = w.take(2 * 2 * D).rearrange("p (u n) -> p u n", u=2)
    msq, rx = m.cols[:, 0:B], m.cols[:, B:2 * B]
    ssk = m.cols[:, 32:64]
    msk = m.cols[:, 224:288].rearrange("p (u h) -> p u h", u=2)
    rqk = m.cols[:, 64:128].rearrange("p (u h) -> p u h", u=2)
    nmax = m.cols[:, 128:136].rearrange("p (a h) -> p a h", a=2)
    rsum = m.cols[:, 160:192].rearrange("p (u h) -> p u h", u=2)
    rinv = m.cols[:, 192:208]
    gq, gk = m.gq, m.gk
    hmask = m.cols[:, 216:224]
    names = ("l1_set l1_raw l1_msq l1_rx l1_xn l1_xnT_ps l1_xnT l1_qk_ps l1_msk l1_rqk l1_qkn "
             "l1_qkT_ps l1_kz l1_v_ps l1_v l1_scores l1_nmax l1_exp l1_pt_ps l1_pts l1_pv l1_oraw l1_rinv l1_rrep "
             "l1_rt_ps l1_rts l1_oT l1_out_ps l1_x l1_vstep l1_gstep").split()
    (set_done, raw_s, msq_s, rx_s, xn_s, xnT_ps, xnT_s, qk_ps, msk_s, rqk_s, qkn_s, qkT_ps, kz_s,
     v_ps, v_s, scores_s, nmax_s, exp_s, pt_ps, pts_s, pv_s, oraw_s, rinv_s, rrep_s, rt_ps, rts_s, oT_s, out_ps, x_s,
     vstep, gstep) = [sem(n) for n in names]
    QK, VB, KTB, SB, TB, OB, RB = 0, 1, 2, 3, 5, 6, 7
    bank = lambda k, lo=0, hi=512: m.ps[:, k, lo:hi]
    head = lambda n, j: 8 * (n // 2) + 2 * j + n % 2

    def bodies(eng, body):
        body(0, first=True)
        with eng.Fori(1, B // 2 - 1) as i:
            body(i)
        body(B // 2 - 1, last=True)

    with nc.Block() as block:
        @block.tensor
        def _(pe):
            pe.sem_inc(pt_ps, 2)
            pe.sem_inc(pv_s, 2)
            pe.wait_ge(m.dma_w[0], 32)

            def turn_x(c):
                pe.wait_ge(xn_s, c + 1)
                if type(c) is int and c < 2:
                    pe.wait_ge(v_s, c)
                else:
                    pe.wait_ge(v_s, c - 1)
                for k in range(KT):
                    mm = nc.tensor.transpose(bank(VB, D + k * P, D + (k + 1) * P), xn[:, k * P:(k + 1) * P], m.ident[:])
                mm.then_inc(xnT_ps, 1)

            def proj_qk(c, u):
                pe.wait_ge(xnT_s, c + 1)
                pe.wait_ge(raw_s, c)
                for k in range(KT):
                    mm = nc.tensor.matmul(bank(QK), xnT[:, u, k], m.w_qkv1[:, k, 0:2 * D], start=(k == 0), stop=(k == KT - 1))
                mm.then_inc(qk_ps, 1)

            def proj_v(c, u, turned):
                pe.wait_ge(xnT_s, turned)
                for k in range(KT):
                    mm = nc.tensor.matmul(bank(VB, 0, D), xnT[:, u, k], m.w_qkv1[:, k, 2 * D:3 * D],
                                          start=(k == 0), stop=(k == KT - 1))
                mm.then_inc(v_ps, 1)

            def turn_qk(c):
                pe.wait_ge(qkn_s, c + 1)
                pe.wait_ge(kz_s, 2 * c)
                for g in range(4):
                    mm = nc.tensor.transpose(bank(KTB, g * P, (g + 1) * P), qkn[:, g * P:(g + 1) * P], m.ident[:])
                mm.then_inc(qkT_ps, 1)

            def scores(c, u, n):
                if n % 2 == 0:
                    pe.wait_ge(kz_s, 2 * c + 1 + n // 2)
                mm = nc.tensor.matmul(bank(SB + n % 2), qT[:, u, n // 2], kz[:, u, n // 2, n % 2:8:2, :], start=True, stop=True)
                mm.then_inc(scores_s, 1)

            def turn_p(c, n):
                pe.wait_ge(exp_s, 4 * c + n + 1)
                pe.wait_ge(pts_s, 4 * c + n)
                for j in range(4):
                    mm = nc.tensor.transpose(bank(TB, j * P, (j + 1) * P), prob[:, n % 2, j * P:(j + 1) * P], m.ident[:])
                mm.then_inc(pt_ps, 1)

            def pv(c, u, n):
                if n == 0:
                    pe.wait_ge(v_s, c + 1)
                    pe.wait_ge(oraw_s, c)
                pe.wait_ge(pts_s, 4 * c + n + 1)
                for j in range(4):
                    h = head(n, j)
                    g = n // 2
                    mm = nc.tensor.matmul(m.ps[32 * j:32 * j + 32, OB, g * P:(g + 1) * P],
                                          vz[:, u, h // 2, 32 * (h % 2):32 * (h % 2) + 32], pts[:, n % 2, j * P:(j + 1) * P],
                                          start=(n % 2 == 0), stop=(n % 2 == 1), tile_position=(0, 32 * j))
                mm.then_inc(pv_s, 1)

            def turn_r(c):
                pe.wait_ge(rrep_s, c + 1)
                pe.wait_ge(x_s, c)
                for g in range(2):
                    mm = nc.tensor.transpose(bank(RB, g * P, (g + 1) * P), rrep[:, g * P:(g + 1) * P], m.ident[:])
                mm.then_inc(rt_ps, 1)

            def out_proj(c):
                pe.wait_ge(oT_s, c + 1)
                nc.tensor.matmul(bank(RB, D, 2 * D), oT[:, 0], m.w_out1[:, 0], start=True, stop=False)
                for g in range(2):
                    nc.tensor.matmul(bank(RB, D + g * P, D + (g + 1) * P), oT[:, g], m.ident[:], start=False, stop=False,
                                     skip_group_check=True)
                mm = nc.tensor.matmul(bank(RB, D, 2 * D), oT[:, 1], m.w_out1[:, 1], start=False, stop=True)
                mm.then_inc(out_ps, 1)

            def stage_a(c, u):
                turn_x(c)
                proj_qk(c, u)

            stage_a(0, 0)
            proj_v(0, 0, 1)
            stage_a(1, 1)
            turn_qk(0)
            scores(0, 0, 0)
            scores(0, 0, 1)

            def body(i, first=False, last=False):
                for u in range(2):
                    b = 2 * i + u
                    head_, tail = first and u == 0, last and u == 1
                    for n in range(4):
                        turn_p(b, n)
                        if n == 0 and not last:
                            turn_x(b + 2)
                        if n == 1 and not head_:
                            turn_r(b - 1)
                        if n < 2:
                            scores(b, u, n + 2)
                        elif not tail:
                            scores(b + 1, 1 - u, n - 2)
                        if n == 1 and not tail:
                            turn_qk(b + 1)
                        if n == 3 and not head_:
                            out_proj(b - 1)
                        pv(b, u, n)
                        if n == 0 and not last:
                            proj_qk(b + 2, u)
                        if n == 1 and not tail:
                            proj_v(b + 1, 1 - u, B if last else b + 3)

            bodies(pe, body)
            turn_r(B - 1)
            out_proj(B - 1)

        @block.scalar
        def _(act):
            def copy_qk(c, u):
                act.wait_ge(qk_ps, c + 1)
                if not (type(c) is int and c < 2):
                    act.wait_ge(qkn_s, c - 1)
                act.wait_ge(msk_s, c)
                nc.scalar.activation(raw[:, u], bank(QK), ACT.Copy)
                nc.scalar.activation(sq, bank(QK), ACT.Square).then_inc(raw_s, 1)

            def copy_v(c, u):
                act.wait_ge(v_ps, c + 1)
                act.wait_ge(set_done, 4)
                src = bank(VB, 0, D).rearrange("p (j r c) -> p j r c", j=8, r=2)
                nc.scalar.activation(vz[:, u, :, 0:DH1], src[:, :, 0], ACT.Copy)
                nc.scalar.activation(vz[:, u, :, 48:48 + DH1], src[:, :, 1], ACT.Copy).then_inc(v_s, 1)

            def exps(c, u, n):
                act.wait_ge(nmax_s, 4 * c + n + 1)
                act.wait_ge(pt_ps, 4 * c + n + 1)
                for j in range(4):
                    h = head(n, j)
                    ins = nc.scalar.activation(prob[:, n % 2, j * P:(j + 1) * P], bank(SB + n % 2, j * P, (j + 1) * P),
                                               ACT.Exp, bias=nmax[:, n % 2, j:j + 1], accum_out=rsum[:, u, h:h + 1])
                ins.then_inc(exp_s, 1)

            def copy_pt(c, n):
                act.wait_ge(pt_ps, 4 * c + n + 3)
                act.wait_ge(pv_s, 4 * c + n + 1)
                nc.scalar.activation(pts[:, n % 2], bank(TB), ACT.Copy).then_inc(pts_s, 1)

            def copy_r(c):
                act.wait_ge(rt_ps, c + 1)
                act.wait_ge(oT_s, c)
                nc.scalar.activation(rts, bank(RB, 0, D), ACT.Copy).then_inc(rts_s, 1)

            copy_qk(0, 0)
            copy_v(0, 0)
            copy_qk(1, 1)
            exps(0, 0, 0)

            def body(i, first=False, last=False):
                for u in range(2):
                    b = 2 * i + u
                    head_, tail = first and u == 0, last and u == 1
                    for n in range(4):
                        if n < 3:
                            exps(b, u, n + 1)
                        elif not tail:
                            exps(b + 1, 1 - u, 0)
                        if n == 1 and not last:
                            copy_qk(b + 2, u)
                        copy_pt(b, n)
                        if n == 1 and not head_:
                            copy_r(b - 1)
                        if n == 2 and not tail:
                            copy_v(b + 1, 1 - u)

            bodies(act, body)
            copy_r(B - 1)

        @block.vector
        def _(dve):
            for u in range(2):
                nc.vector.memset(vz[:, u], 0.0).then_inc(set_done, 1)
            dve.wait_ge(m.small_loaded, 16 * SMALL)
            dve.wait_ge(set_done, 3)
            nc.vector.tensor_scalar(gq, gq, float(DH1) ** -0.5, None, ALU.mult).then_inc(set_done, 1)
            nc.vector.tensor_scalar(hmask, hmask, gk, None, ALU.mult).then_inc(vstep, 1)
            dve.wait_ge(set_done, 4)
            dve.wait_ge(vstep, 1)

            def mean_x(c0, c1, k):
                nc.vector.tensor_scalar(msq[:, c0:c1], m.ssq[:, c0:c1], 1.0 / D, EPS, ALU.mult, ALU.add).then_inc(msq_s, 1)

            def norm_x(c):
                dve.wait_ge(xnT_ps, c)
                nc.vector.tensor_scalar(xn, row(m.X, c), rx[:, bass.ds(c, 1)], None, ALU.mult).then_inc(xn_s, 1)

            def modulate(c, u):
                dve.wait_ge(xnT_ps, c + 1)
                for k in range(KT):
                    ins = nc.vector.tensor_scalar(xnT[:, u, k], bank(VB, D + k * P, D + (k + 1) * P), col(m.A1, k, c),
                                                  col(m.mod1, KT + k, c), ALU.mult, ALU.add)
                ins.then_inc(xnT_s, 1)

            def mean_qk(c, u):
                dve.wait_ge(raw_s, c + 1)
                if not (type(c) is int and c < 2):
                    dve.wait_ge(rqk_s, c - 1)
                nc.vector.tensor_reduce(ssk, sq.rearrange("p (h d) -> p h d", d=DH1), AX.X, ALU.add).then_inc(vstep, 1)
                dve.wait_ge(vstep, c + 2)
                nc.vector.tensor_scalar(msk[:, u], ssk, 1.0 / DH1, EPS, ALU.mult, ALU.add).then_inc(msk_s, 1)

            def norm_qk(c, u):
                dve.wait_ge(rqk_s, c + 1)
                dve.wait_ge(qkT_ps, c)
                nc.vector.tensor_tensor(qkn.rearrange("p (h d) -> p h d", d=DH1), raw[:, u].rearrange("p (h d) -> p h d", d=DH1),
                                        rqk[:, u].unsqueeze(2).broadcast_to([P, 2 * H, DH1]), ALU.mult).then_inc(qkn_s, 1)

            def spread_q(c, u):
                dve.wait_ge(qkT_ps, c + 1)
                nc.vector.tensor_scalar(qT[:, u], bank(KTB, 0, 2 * P).rearrange("p (g t) -> p g t", g=2), gq, None, ALU.mult)

            def spread_k(c, u, g):
                nc.vector.tensor_tensor(kz[:, u, g], bank(KTB, (2 + g) * P, (3 + g) * P).unsqueeze(1).broadcast_to([P, 8, P]),
                                        hmask.unsqueeze(2).broadcast_to([P, 8, P]), ALU.mult).then_inc(kz_s, 1)

            def maxes(c, n):
                dve.wait_ge(scores_s, 4 * c + n + 1)
                nc.vector.tensor_reduce(nmax[:, n % 2], bank(SB + n % 2).rearrange("p (h t) -> p h t", h=4), AX.X, ALU.max,
                                        negate=True).then_inc(nmax_s, 1)

            def recip(c, u):
                dve.wait_ge(exp_s, 4 * (c + 1))
                dve.wait_ge(rrep_s, c)
                nc.vector.reciprocal(rinv, rsum[:, u]).then_inc(rinv_s, 1)

            def take_o(c):
                dve.wait_ge(pv_s, 4 * (c + 1) + 2)
                dve.wait_ge(oT_s, c)
                nc.vector.tensor_copy(oraw, bank(OB, 0, D)).then_inc(oraw_s, 1)

            def norm_o(c):
                dve.wait_ge(rts_s, c + 1)
                dve.wait_ge(oraw_s, c + 1)
                dve.wait_ge(out_ps, c)
                nc.vector.tensor_tensor(oT.rearrange("p g t -> p (g t)"), oraw, rts, ALU.mult).then_inc(oT_s, 1)

            def add(c):
                dve.wait_ge(out_ps, c + 1)
                nc.vector.tensor_tensor(row(m.X, c), row(m.X, c), bank(RB, D, 2 * D), ALU.add).then_inc(x_s, 1)

            mean_x(0, 2, 0)
            mean_x(2, B, 1)
            dve.wait_ge(rx_s, 1)
            norm_x(0)
            modulate(0, 0)
            norm_x(1)
            modulate(1, 1)
            mean_qk(0, 0)
            mean_qk(1, 1)
            norm_qk(0, 0)
            spread_q(0, 0)
            spread_k(0, 0, 0)
            spread_k(0, 0, 1)
            maxes(0, 0)
            dve.wait_ge(rx_s, 2)

            def body(i, first=False, last=False):
                for u in range(2):
                    b = 2 * i + u
                    head_, tail = first and u == 0, last and u == 1
                    for n in range(4):
                        if n < 3:
                            maxes(b, n + 1)
                        elif not tail:
                            maxes(b + 1, 0)
                        if n == 0 and not last:
                            norm_x(b + 2)
                        if n == 0 and not head_:
                            recip(b - 1, 1 - u)
                        if n == 0 and not first:
                            add(b - 2)
                        if n == 0 and not last:
                            modulate(b + 2, u)
                        if n == 0 and not head_:
                            take_o(b - 1)
                        if n == 1 and not tail:
                            norm_qk(b + 1, 1 - u)
                        if n == 1 and not tail:
                            spread_q(b + 1, 1 - u)
                            spread_k(b + 1, 1 - u, 0)
                        if n == 2 and not last:
                            mean_qk(b + 2, u)
                        if n == 2 and not tail:
                            spread_k(b + 1, 1 - u, 1)
                        if n == 2 and not head_:
                            norm_o(b - 1)

            bodies(dve, body)
            recip(B - 1, 1)
            take_o(B - 1)
            add(B - 2)
            norm_o(B - 1)
            add(B - 1)

        @block.gpsimd
        def _(pool):
            c = Chain(pool, gstep)
            c.link(nc.gpsimd.memset(hmask, 1.0))
            c.link(nc.gpsimd.affine_select(out=hmask, in_=hmask, compare_op=ALU.is_ge, fill=0.0, base=0,
                                           pattern=[[-DH1, 8]], channel_multiplier=1))
            nc.gpsimd.affine_select(out=hmask, in_=hmask, compare_op=ALU.is_ge, fill=0.0, base=DH1 - 1,
                                    pattern=[[DH1, 8]], channel_multiplier=-1).then_inc(set_done, 1)

            def pow_x(c0, c1, k):
                pool.wait_ge(msq_s, k + 1)
                nc.gpsimd.tensor_tensor(rx[:, c0:c1], msq[:, c0:c1], m.nhalf[:, c0:c1], ALU.pow).then_inc(rx_s, 1)

            def pow_qk(c, u):
                pool.wait_ge(msk_s, c + 1)
                if not (type(c) is int and c < 2):
                    pool.wait_ge(qkn_s, c - 1)
                nc.gpsimd.tensor_tensor(rqk[:, u], msk[:, u], m.nhalf[:], ALU.pow).then_inc(rqk_s, 1)

            def spread(c):
                pool.wait_ge(rinv_s, c + 1)
                pool.wait_ge(rt_ps, c)
                carry(pool, m)
                nc.gpsimd.tensor_copy(rrep.rearrange("p (h d) -> p h d", d=DH1),
                                      rinv.unsqueeze(2).broadcast_to([P, H, DH1])).then_inc(rrep_s, 1)

            pow_x(0, 2, 0)
            pow_qk(0, 0)
            pow_qk(1, 1)
            pow_x(2, B, 1)

            def body(i, first=False, last=False):
                for u in range(2):
                    b = 2 * i + u
                    head_ = first and u == 0
                    if not head_:
                        spread(b - 1)
                    if not last:
                        pow_qk(b + 2, u)

            bodies(pool, body)
            spread(B - 1)


def phase_l2(nc, a, m, sem):
    w = Space(m.work)
    xn = w.take(D)
    x1T = w.take(KT * P).rearrange("p (k t) -> p k t", k=KT)
    qT = w.take(4 * P).rearrange("p (h t) -> p h t", h=4)
    kT = w.take(4 * P).rearrange("p (h t) -> p h t", h=4)
    vv = w.take(2 * 4 * P).rearrange("p (a n) -> p a n", a=2)
    prob = w.take(4 * P).rearrange("p (h t) -> p h t", h=4)
    pn = w.take(4 * P).rearrange("p (h t) -> p h t", h=4)
    pts = w.take(4 * P).rearrange("p (h t) -> p h t", h=4)
    oT = w.take(4 * P).rearrange("p (h t) -> p h t", h=4)
    ao = w.take(KT * P).rearrange("p (k t) -> p k t", k=KT)
    stats = m.cols[:, 0:6]
    mv = m.cols[:, 8:10]
    var, rstd = m.cols[:, 10:11], m.cols[:, 11:12]
    nmax = m.cols[:, 16:20]
    rsum = m.cols[:, 24:28]
    rinv = m.cols[:, 32:36]
    bq = m.bq
    wqkv = m.big[:].rearrange("p (k g n) -> p k g n", k=KT, g=3)
    wo = m.ring[:, 0:4096].rearrange("p (h n) -> p h n", h=H)
    names = ("l2_var l2_rstd l2_xn l2_xT_ps l2_x1T l2_q_ps l2_k_ps l2_v_ps l2_q l2_k l2_v l2_scores "
             "l2_nmax l2_exp l2_rinv l2_pn l2_pt_ps l2_pts l2_pv l2_oT l2_out_ps l2_ao l2_back_ps l2_x l2_vstep").split()
    (var_s, rstd_s, xn_s, xT_ps, x1T_s, q_ps, k_ps, v_ps, q_s, k_s, v_s, scores_s, nmax_s, exp_s, rinv_s,
     pn_s, pt_ps, pts_s, pv_s, oT_s, out_ps, ao_s, back_ps, x_s, vstep) = [sem(n) for n in names]
    QB, KB, VB, SB, TB, OB, AB = 0, 1, 2, 3, 4, 5, 6
    bank = lambda k, lo=0, hi=512: m.ps[:, k, lo:hi]
    four = lambda v: v.rearrange("p (h t) -> p h t", h=4)

    def bodies(eng, body):
        body(0, first=True)
        with eng.Fori(1, B - 1) as b:
            body(b)
        body(B - 1, last=True)

    with nc.Block() as block:
        @block.tensor
        def _(pe):
            def turn_x(c):
                pe.wait_ge(xn_s, c + 1)
                for k in range(KT):
                    mm = nc.tensor.transpose(bank(SB, k * P, (k + 1) * P), xn[:, k * P:(k + 1) * P], m.ident[:])
                mm.then_inc(xT_ps, 1)

            def project(b, g):
                n = 4 * b + g
                if g == 0:
                    pe.wait_ge(x1T_s, b + 1)
                pe.wait_ge(q_s, n)
                for h in range(4):
                    for k in range(KT):
                        mm = nc.tensor.matmul(bank(QB, h * P, (h + 1) * P), wqkv[:, k, 0, (4 * g + h) * P:(4 * g + h + 1) * P],
                                              x1T[:, k], start=(k == 0), stop=(k == KT - 1))
                mm.then_inc(q_ps, 1)
                pe.wait_ge(k_s, n)
                for h in range(4):
                    for k in range(KT):
                        mm = nc.tensor.matmul(bank(KB, h * P, (h + 1) * P), wqkv[:, k, 1, (4 * g + h) * P:(4 * g + h + 1) * P],
                                              x1T[:, k], start=(k == 0), stop=(k == KT - 1))
                mm.then_inc(k_ps, 1)
                pe.wait_ge(v_s, n)
                for k in range(KT):
                    mm = nc.tensor.matmul(bank(VB), x1T[:, k], wqkv[:, k, 2, 4 * g * P:(4 * g + 4) * P],
                                          start=(k == 0), stop=(k == KT - 1))
                mm.then_inc(v_ps, 1)

            def scores(b, g):
                n = 4 * b + g
                pe.wait_ge(q_s, n + 1)
                pe.wait_ge(k_s, n + 1)
                for h in range(4):
                    mm = nc.tensor.matmul(bank(SB, h * P, (h + 1) * P), qT[:, h], kT[:, h], start=True, stop=True)
                mm.then_inc(scores_s, 1)

            def turn_p(b, g):
                n = 4 * b + g
                pe.wait_ge(pn_s, n + 1)
                pe.wait_ge(pts_s, n)
                for h in range(4):
                    mm = nc.tensor.transpose(bank(TB, h * P, (h + 1) * P), pn[:, h], m.ident[:])
                mm.then_inc(pt_ps, 1)

            def pv(b, g):
                n = 4 * b + g
                pe.wait_ge(pts_s, n + 1)
                pe.wait_ge(v_s, n + 1)
                pe.wait_ge(oT_s, n)
                for h in range(4):
                    mm = nc.tensor.matmul(bank(OB, h * P, (h + 1) * P), vv[:, g % 2, h * P:(h + 1) * P], pts[:, h],
                                          start=True, stop=True)
                mm.then_inc(pv_s, 1)

            def out_proj(b, g):
                n = 4 * b + g
                pe.wait_ge(oT_s, n + 1)
                if g == 0:
                    pe.wait_ge(ao_s, b)
                for h in range(4):
                    for k in range(KT):
                        mm = nc.tensor.matmul(bank(AB + k, 0, P), wo[:, 4 * g + h, k * P:(k + 1) * P], oT[:, h],
                                              start=(g == 0 and h == 0), stop=(g == 3 and h == 3))
                mm.then_inc(out_ps, 1)

            def turn_back(b):
                pe.wait_ge(ao_s, b + 1)
                for k in range(KT):
                    mm = nc.tensor.transpose(bank(SB, k * P, (k + 1) * P), ao[:, k], m.ident[:])
                mm.then_inc(back_ps, 1)

            pe.wait_ge(m.dma_w[2], 16)
            pe.wait_ge(m.dma_w[3], 48)
            turn_x(0)
            project(0, 0)

            def body(b, first=False, last=False):
                for g in range(4):
                    if g == 3 and not last:
                        pe.wait_ge(x1T_s, b + 2)
                    if g == 2 and not first:
                        pe.wait_ge(x_s, b)
                    scores(b, g)
                    if g < 3:
                        project(b, g + 1)
                    elif not last:
                        project(b + 1, 0)
                    turn_p(b, g)
                    if g == 2 and not last:
                        turn_x(b + 1)
                    if g == 1 and not first:
                        turn_back(b - 1)
                    if g > 0:
                        out_proj(b, g - 1)
                    elif not first:
                        out_proj(b - 1, 3)
                    pv(b, g)

            bodies(pe, body)
            out_proj(B - 1, 3)
            turn_back(B - 1)

        @block.scalar
        def _(act):
            def copy_v(b, g):
                n = 4 * b + g
                act.wait_ge(v_ps, n + 1)
                nc.scalar.activation(vv[:, g % 2], bank(VB), ACT.Copy).then_inc(v_s, 1)

            def exps(b, g):
                n = 4 * b + g
                act.wait_ge(nmax_s, n + 1)
                act.wait_ge(pn_s, n)
                for h in range(4):
                    ins = nc.scalar.activation(prob[:, h], bank(SB, h * P, (h + 1) * P), ACT.Exp, bias=nmax[:, h:h + 1],
                                               accum_out=rsum[:, h:h + 1])
                ins.then_inc(exp_s, 1)

            def copy_pt(b, g):
                n = 4 * b + g
                act.wait_ge(pt_ps, n + 1)
                act.wait_ge(pv_s, n)
                nc.scalar.activation(pts.rearrange("p h t -> p (h t)"), bank(TB), ACT.Copy).then_inc(pts_s, 1)

            copy_v(0, 0)

            def body(b, first=False, last=False):
                for g in range(4):
                    exps(b, g)
                    if g < 3:
                        copy_v(b, g + 1)
                    elif not last:
                        copy_v(b + 1, 0)
                    copy_pt(b, g)

            bodies(act, body)

        @block.vector
        def _(dve):
            dve.wait_ge(m.small_loaded, 16 * SMALL)
            nc.vector.tensor_scalar(bq[:, 0:H], bq[:, 0:H], SCALE2, None, ALU.mult).then_inc(vstep, 1)
            dve.wait_ge(vstep, 1)

            def stats_x(c):
                nc.vector.bn_stats(stats, row(m.X, c)).then_inc(vstep, 1)
                dve.wait_ge(vstep, 2 * c + 2)
                carry(dve, m)
                nc.vector.bn_aggr(mv, stats).then_inc(vstep, 1)
                dve.wait_ge(vstep, 2 * c + 3)
                nc.vector.tensor_scalar(var, mv[:, 1:2], EPS, None, ALU.add).then_inc(var_s, 1)

            def norm_x(c):
                dve.wait_ge(rstd_s, c + 1)
                nc.vector.tensor_scalar(xn, row(m.X, c), mv[:, 0:1], rstd, ALU.subtract, ALU.mult).then_inc(xn_s, 1)

            def modulate(c):
                dve.wait_ge(xT_ps, c + 1)
                for k in range(KT):
                    ins = nc.vector.tensor_scalar(x1T[:, k], bank(SB, k * P, (k + 1) * P), col(m.ada, KT + k, c),
                                                  col(m.ada, k, c), ALU.mult, ALU.add)
                ins.then_inc(x1T_s, 1)

            def copy_qk(b, g):
                n = 4 * b + g
                dve.wait_ge(q_ps, n + 1)
                nc.vector.scalar_tensor_tensor(out=qT, in0=four(bank(QB)), scalar=SCALE2,
                                               in1=bq[:, 4 * g:4 * g + 4].unsqueeze(2).broadcast_to([P, 4, P]),
                                               op0=ALU.mult, op1=ALU.add).then_inc(q_s, 1)
                dve.wait_ge(k_ps, n + 1)
                nc.vector.tensor_tensor(kT, four(bank(KB)), bq[:, H + 4 * g:H + 4 * g + 4].unsqueeze(2).broadcast_to([P, 4, P]),
                                        ALU.add).then_inc(k_s, 1)

            def maxes(b, g):
                n = 4 * b + g
                dve.wait_ge(scores_s, n + 1)
                nc.vector.tensor_reduce(nmax, four(bank(SB)), AX.X, ALU.max, negate=True).then_inc(nmax_s, 1)

            def recip(b, g):
                n = 4 * b + g
                dve.wait_ge(exp_s, n + 1)
                nc.vector.reciprocal(rinv, rsum).then_inc(rinv_s, 1)

            def copy_o(b, g):
                n = 4 * b + g
                dve.wait_ge(pv_s, n + 1)
                dve.wait_ge(out_ps, n)
                nc.vector.tensor_tensor(oT, four(bank(OB)), bq[:, 2 * H + 4 * g:2 * H + 4 * g + 4].unsqueeze(2).broadcast_to([P, 4, P]),
                                        ALU.add).then_inc(oT_s, 1)

            def gate(b):
                dve.wait_ge(out_ps, 4 * (b + 1))
                for k in range(KT):
                    ins = nc.vector.tensor_scalar(ao[:, k], bank(AB + k, 0, P), col(m.ada, 2 * KT + k, b), col(m.gb, k, b),
                                                  ALU.mult, ALU.add)
                ins.then_inc(ao_s, 1)

            def add(b):
                dve.wait_ge(back_ps, b + 1)
                nc.vector.tensor_tensor(row(m.XA, b), row(m.X, b), bank(SB, 0, D), ALU.add).then_inc(x_s, 1)

            stats_x(0)
            norm_x(0)
            modulate(0)
            copy_qk(0, 0)

            def body(b, first=False, last=False):
                for g in range(4):
                    maxes(b, g)
                    recip(b, g)
                    if g == 0 and not last:
                        stats_x(b + 1)
                    if g == 1 and not last:
                        norm_x(b + 1)
                    if g < 3:
                        copy_qk(b, g + 1)
                    elif not last:
                        copy_qk(b + 1, 0)
                    if g == 2 and not last:
                        modulate(b + 1)
                    if g == 1 and not first:
                        add(b - 1)
                    if g == 0 and not first:
                        gate(b - 1)
                    copy_o(b, g)

            bodies(dve, body)
            gate(B - 1)
            add(B - 1)

        @block.gpsimd
        def _(pool):
            def pow_x(c):
                pool.wait_ge(var_s, c + 1)
                pool.wait_ge(xn_s, c)
                nc.gpsimd.tensor_tensor(rstd, var, m.nhalf[:, 0:1], ALU.pow).then_inc(rstd_s, 1)

            def normalise(b, g):
                n = 4 * b + g
                pool.wait_ge(rinv_s, n + 1)
                pool.wait_ge(pt_ps, n)
                nc.gpsimd.tensor_tensor(pn, prob, rinv.unsqueeze(2).broadcast_to([P, 4, P]), ALU.mult).then_inc(pn_s, 1)

            def both(b):
                pool.wait_ge(x_s, b + 1)
                nc.gpsimd.tensor_tensor(row(m.X, b), row(m.X, b), row(m.XA, b), ALU.add)

            pow_x(0)

            def body(b, first=False, last=False):
                for g in range(4):
                    normalise(b, g)
                    if g == 0 and not last:
                        pow_x(b + 1)
                    if g == 2 and not first:
                        both(b - 1)

            bodies(pool, body)
            both(B - 1)


def phase_ffn(nc, a, m, sem):
    w = Space(m.work)
    GB = 4
    GT = GB * P
    NG = B // GB
    MC = MLP // P
    xn = w.take(GB * D).rearrange("p (b d) -> p b d", b=GB)
    x2T = w.take(KT * GT).rearrange("p (k t) -> p k t", k=KT)
    hT = w.take(MC * GT).rearrange("p (c t) -> p c t", c=MC)
    fo = w.take(KT * GT).rearrange("p (k t) -> p k t", k=KT)
    x3 = w.take(GB * D).rearrange("p (b d) -> p b d", b=GB)
    x3T = w.take(KT * GT).rearrange("p (k t) -> p k t", k=KT)
    stats = m.cols[:, 0:24].rearrange("p (b s) -> p b s", b=GB)
    mv = m.cols[:, 24:32].rearrange("p (b s) -> p b s", b=GB)
    var, rstd = m.cols[:, 32:36], m.cols[:, 36:40]
    b1, bih, bhh = m.b1, m.bih, m.bhh
    bg = m.cols[:, 80:86]
    m.bhh_n = m.bhh[:, 4:6]
    w1 = m.ring[:, 4096:6144].rearrange("p (k n) -> p k n", k=KT)
    w2 = m.ring[:, 6144:8192].rearrange("p (c n) -> p c n", c=MC)
    gi = m.big[:].rearrange("p (t c b) -> p c b t", c=GATES, b=B)
    whh = m.w_qkv1[:].rearrange("p k n -> p (k n)")
    whp = m.whp[:].rearrange("p a k n -> p a (k n)")
    m.split, whh_loaded, gstep = sem("whh_split"), sem("ff_whh_loaded"), sem("ff_gstep")
    names = ("ff_var ff_rstd ff_xn ff_xT_ps ff_x2T ff_h_ps ff_h ff_o_ps ff_fo ff_back_ps ff_x3 ff_x3T_ps "
             "ff_x3T ff_gi_ps ff_gi ff_vstep ff_bg ff_x").split()
    (var_s, rstd_s, xn_s, xT_ps, x2T_s, h_ps, h_s, o_ps, fo_s, back_ps, x3_s, x3T_ps, x3T_s, gi_ps, gi_s,
     vstep, bg_s, x_s) = [sem(n) for n in names]
    HB, XB, OB, RB = 0, 2, 4, 6
    bank = lambda k, lo=0, hi=512: m.ps[:, k, lo:hi]

    def bodies(eng, body):
        for g in range(NG):
            body(g, first=g == 0, last=g == NG - 1)

    with nc.Block() as block:
        @block.sync
        def _(sp):
            sp.dma_start(m.w_qkv1[:], a["L3_cond_W_hh"].rearrange("(k p) n -> p k n", p=P)).then_inc(whh_loaded, 16)

        @block.tensor
        def _(pe):
            def turn_x(g):
                pe.wait_ge(xn_s, g + 1)
                pe.wait_ge(x3T_s, g - 1) if not (type(g) is int and g == 0) else None
                for k in range(KT):
                    for b in range(GB):
                        mm = nc.tensor.transpose(bank(XB + k, b * P, (b + 1) * P), xn[:, b, k * P:(k + 1) * P], m.ident[:])
                mm.then_inc(xT_ps, 1)

            def up(g, c):
                if c == 0:
                    pe.wait_ge(x2T_s, g + 1)
                if c == 0 and not (type(g) is int and g == 0):
                    pe.wait_ge(gi_s, GATES * (g - 1))
                if c >= 2:
                    pe.wait_ge(h_s, MC * g + c - 1)
                for k in range(KT):
                    mm = nc.tensor.matmul(bank(HB + c % 2), w1[:, k, c * P:(c + 1) * P], x2T[:, k], start=(k == 0), stop=(k == KT - 1))
                mm.then_inc(h_ps, 1)

            def down(g):
                pe.wait_ge(fo_s, g)
                for c in range(MC):
                    pe.wait_ge(h_s, MC * g + c + 1)
                    for k in range(KT):
                        mm = nc.tensor.matmul(bank(OB + k), w2[:, c, k * P:(k + 1) * P], hT[:, c], start=(c == 0), stop=(c == MC - 1))
                mm.then_inc(o_ps, 1)

            def turn_back(g):
                pe.wait_ge(fo_s, g + 1)
                pe.wait_ge(x3_s, g)
                for b in range(GB):
                    for k in range(KT):
                        mm = nc.tensor.transpose(bank(RB + b // 2, (b % 2) * D + k * P, (b % 2) * D + (k + 1) * P),
                                                 fo[:, k, b * P:(b + 1) * P], m.ident[:])
                mm.then_inc(back_ps, 1)

            def turn_x3(g, last=False):
                pe.wait_ge(x3_s, g + 1)
                pe.wait_ge(x2T_s, g + 1 if last else g + 2)
                for k in range(KT):
                    for b in range(GB):
                        mm = nc.tensor.transpose(bank(XB + k, b * P, (b + 1) * P), x3[:, b, k * P:(k + 1) * P], m.ident[:])
                mm.then_inc(x3T_ps, 1)

            def gates(g, last=False):
                pe.wait_ge(x3T_s, g + 1)
                pe.wait_ge(h_s, MC * (g + 1) if last else MC * (g + 2))
                for c in range(GATES):
                    if c >= 2:
                        pe.wait_ge(gi_s, GATES * g + c - 1)
                    for k in range(KT):
                        mm = nc.tensor.matmul(bank(HB + c % 2), m.w_ih[:, k, c * P:(c + 1) * P], x3T[:, k], start=(k == 0), stop=(k == KT - 1))
                    mm.then_inc(gi_ps, 1)

            pe.wait_ge(m.dma_w[1], 16)
            turn_x(0)

            def body(g, first=False, last=False):
                for c in range(MC):
                    up(g, c)
                    if c == 3 and not first:
                        turn_back(g - 1)
                if not first:
                    turn_x3(g - 1)
                down(g)
                if not last:
                    turn_x(g + 1)
                if not first:
                    gates(g - 1)

            bodies(pe, body)
            turn_back(NG - 1)
            turn_x3(NG - 1, last=True)
            gates(NG - 1, last=True)

        @block.scalar
        def _(act):
            act.wait_ge(m.small_loaded, 16 * SMALL)
            act.wait_ge(bg_s, 1)

            def gelus(g):
                for c in range(MC):
                    act.wait_ge(h_ps, MC * g + c + 1)
                    if c == 0:
                        act.wait_ge(o_ps, g)
                    nc.scalar.activation(hT[:, c], bank(HB + c % 2), ACT.Gelu, bias=b1[:, c:c + 1]).then_inc(h_s, 1)

            def copy_x3(g):
                act.wait_ge(x3T_ps, g + 1)
                act.wait_ge(gi_ps, GATES * g)
                for k in range(KT):
                    ins = nc.scalar.activation(x3T[:, k], bank(XB + k), ACT.Copy)
                ins.then_inc(x3T_s, 1)

            def copy_gates(g):
                for c in range(GATES):
                    act.wait_ge(gi_ps, GATES * g + c + 1)
                    nc.scalar.activation(gi[:, c, bass.ds(GB * g, GB), :], bank(HB + c % 2).rearrange("p (b t) -> p b t", b=GB),
                                         ACT.Identity, bias=bg[:, c:c + 1]).then_inc(gi_s, 1)

            def body(g, first=False, last=False):
                gelus(g)
                if not first:
                    copy_x3(g - 1)
                    copy_gates(g - 1)

            bodies(act, body)
            copy_x3(NG - 1)
            copy_gates(NG - 1)

        @block.vector
        def _(dve):
            dve.wait_ge(m.small_loaded, 16 * SMALL)
            nc.vector.tensor_tensor(bg[:, 0:4], bih[:, 0:4], bhh[:, 0:4], ALU.add)
            nc.vector.tensor_copy(bg[:, 4:6], bih[:, 4:6]).then_inc(bg_s, 1)

            def norm_x(g):
                for b in range(GB):
                    ins = nc.vector.bn_stats(stats[:, b], row(m.XA, GB * g + b))
                ins.then_inc(vstep, 1)
                dve.wait_ge(vstep, 2 * g + 1)
                carry(dve, m)
                for b in range(GB):
                    ins = nc.vector.bn_aggr(mv[:, b], stats[:, b])
                ins.then_inc(vstep, 1)
                dve.wait_ge(vstep, 2 * g + 2)
                nc.vector.tensor_scalar(var, mv[:, :, 1], EPS, None, ALU.add).then_inc(var_s, 1)
                dve.wait_ge(rstd_s, g + 1)
                dve.wait_ge(xT_ps, g)
                for b in range(GB):
                    ins = nc.vector.tensor_scalar(xn[:, b], row(m.XA, GB * g + b), mv[:, b, 0:1], rstd[:, b:b + 1],
                                                  ALU.subtract, ALU.mult)
                ins.then_inc(xn_s, 1)

            def modulate(g):
                dve.wait_ge(xT_ps, g + 1)
                dve.wait_ge(h_ps, MC * g)
                for k in range(KT):
                    for b in range(GB):
                        ins = nc.vector.tensor_scalar(x2T[:, k, b * P:(b + 1) * P], bank(XB + k, b * P, (b + 1) * P),
                                                      col(m.ada, 4 * KT + k, GB * g + b), col(m.ada, 3 * KT + k, GB * g + b),
                                                      ALU.mult, ALU.add)
                ins.then_inc(x2T_s, 1)

            def gate(g):
                dve.wait_ge(o_ps, g + 1)
                dve.wait_ge(back_ps, g)
                for k in range(KT):
                    for b in range(GB):
                        ins = nc.vector.tensor_scalar(fo[:, k, b * P:(b + 1) * P], bank(OB + k, b * P, (b + 1) * P),
                                                      col(m.ada, 5 * KT + k, GB * g + b), col(m.gb, 2 + k, GB * g + b),
                                                      ALU.mult, ALU.add)
                ins.then_inc(fo_s, 1)

            def add(g):
                dve.wait_ge(back_ps, g + 1)
                dve.wait_ge(x3T_ps, g)
                dve.wait_ge(x_s, g)
                for h in range(2):
                    ins = nc.vector.tensor_tensor(x3[:, 2 * h:2 * h + 2], m.X[:, bass.ds(GB * g + 2 * h, 2), :],
                                                  bank(RB + h).rearrange("p (b d) -> p b d", b=2), ALU.add)
                ins.then_inc(x3_s, 1)

            norm_x(0)
            modulate(0)

            def body(g, first=False, last=False):
                if not first:
                    add(g - 1)
                if not last:
                    norm_x(g + 1)
                    modulate(g + 1)
                gate(g)

            bodies(dve, body)
            add(NG - 1)

        @block.gpsimd
        def _(pool):
            def pow_x(g):
                pool.wait_ge(var_s, g + 1)
                pool.wait_ge(xn_s, g)
                nc.gpsimd.tensor_tensor(rstd, var, m.nhalf[:, 0:GB], ALU.pow).then_inc(rstd_s, 1)

            def store(g):
                pool.wait_ge(x3_s, g + 1)
                carry(pool, m)
                nc.gpsimd.tensor_copy(m.X[:, bass.ds(GB * g, GB), :], x3).then_inc(x_s, 1)

            pow_x(0)

            def split_whh():
                c = Chain(pool, gstep)
                pool.wait_ge(whh_loaded, 16)
                c.link(nc.gpsimd.tensor_copy(whp[:, 0], whh))
                c.link(nc.gpsimd.tensor_tensor(whh, whh, whp[:, 0], ALU.subtract))
                c.link(nc.gpsimd.tensor_copy(whp[:, 1], whh))
                nc.gpsimd.tensor_tensor(whp[:, 2], whh, whp[:, 1], ALU.subtract).then_inc(m.split, 1)

            def body(g, first=False, last=False):
                if not first:
                    store(g - 1)
                if not last:
                    pow_x(g + 1)
                if first:
                    split_whh()

            bodies(pool, body)
            store(NG - 1)


def phase_gru(nc, a, m, sem, out):
    w = Space(m.work)
    hp = w.take(2 * KT * NPART * B, BF16).rearrange("p (u k n) -> p u k n", u=2, k=KT)
    h = w.take(2 * KT * B).rearrange("p (u k b) -> p u k b", u=2, k=KT)
    rest = w.take(KT * B).rearrange("p (k b) -> p k b", k=KT)
    pre = w.take(GATES * B).rearrange("p (c b) -> p c b", c=GATES)
    act_out = w.take(GATES * B).rearrange("p (c b) -> p c b", c=GATES)
    zh = w.take(KT * B).rearrange("p (k b) -> p k b", k=KT)
    mn = w.take(KT * B).rearrange("p (k b) -> p k b", k=KT)
    rn = w.take(KT * B).rearrange("p (k b) -> p k b", k=KT)
    npre = w.take(KT * B).rearrange("p (k b) -> p k b", k=KT)
    bn = w.take(KT * B).rearrange("p (k b) -> p k b", k=KT)
    hist = w.take(KT * B * N).rearrange("p (k b t) -> p k b t", k=KT, b=B)
    res = w.take(2 * 512).rearrange("p (a n) -> p a n", a=2)
    gi = m.big[:].rearrange("p (t n) -> p t n", t=N)
    names = ("gru_h gru_r_ps gru_n_ps gru_z_ps gru_r_pre gru_z_pre gru_n_sum gru_n_pre gru_bn gru_r gru_z gru_n gru_step gru_state "
             "gru_rest gru_kept gru_turned gru_summed gru_stored0 gru_stored1").split()
    (h_s, r_ps, n_ps, z_ps, r_pre, z_pre, n_sum, n_pre, bn_s, r_s, z_s, n_s, step, state_s, rest_s, kept, turned, summed,
     *stored) = [sem(n) for n in names]
    RB, NB, ZB = 0, 1, 2
    LINKS = 3
    hparts = lambda u, j: hp[:, u].rearrange("p k (a b) -> p k a b", a=NPART)[:, :, j]
    parts_sum = lambda k: m.ps[:, k, 0:96].rearrange("p (c a b) -> p c b a", c=KT, a=NPART)

    def steps(eng, body):
        with eng.Fori(0, N // UNROLL) as i:
            for s in range(UNROLL):
                body(UNROLL * i + s, s % 2)

    with nc.Block() as block:
        @block.tensor
        def _(pe):
            pe.wait_ge(m.split, 1)

            pe.wait_ge(bn_s, 1)

            def time_step(t, u):
                for _ in range(IDLE):
                    nc.tensor.matmul(m.ps[:, 7], m.identb[:], m.whp[:, 0, 0, 0:512], start=True, stop=True)
                first = lambda k: m.ps[:, k, 0:96].rearrange("p (c a b) -> p c a b", c=KT, a=NPART)[:, :, 0]
                gate = lambda k: gi[:, bass.ds(t, 1), 2 * k * B:2 * (k + 1) * B].rearrange("p o n -> p (o n)")
                for bk, read, add in ((RB, r_pre, gate(0)), (NB, n_sum, bn.rearrange("p c b -> p (c b)")), (ZB, z_pre, gate(1))):
                    pe.wait_ge(read, t + 1)
                    nc.tensor.matmul(first(bk), m.ident[:], add, start=True, stop=False, skip_group_check=True)
                pe.wait_ge(h_s, t + 1)
                for bk, c0, done in ((RB, 0, r_ps), (NB, 4, n_ps), (ZB, 2, z_ps)):
                    for c in range(KT):
                        for k in range(KT):
                            for j in range(NPART):
                                mm = nc.tensor.matmul(m.ps[:, bk, 48 * c:48 * c + 48],
                                                      m.whp[:, j, k, (c0 + c) * P:(c0 + c + 1) * P], hp[:, u, k],
                                                      start=False, stop=(k == KT - 1 and j == NPART - 1), skip_group_check=True)
                    mm.then_inc(done, 1)

            steps(pe, time_step)
            pe.wait_ge(kept, N + 2)
            for q in range(B // 2):
                if q >= 4:
                    pe.wait_ge(summed, q - 3)
                for b in range(2):
                    for k in range(KT):
                        mm = nc.tensor.transpose(m.ps[:, 4 + q % 4, b * D + k * P:b * D + (k + 1) * P], hist[:, k, 2 * q + b],
                                                 m.ident[:])
                mm.then_inc(turned, 1)

        @block.scalar
        def _(act):
            def time_step(t, u):
                act.wait_ge(r_pre, t + 2)
                nc.scalar.activation(act_out[:, 0:2], pre[:, 0:2], ACT.Sigmoid).then_inc(r_s, 1)
                act.wait_ge(z_pre, t + 2)
                nc.scalar.activation(act_out[:, 2:4], pre[:, 2:4], ACT.Sigmoid).then_inc(z_s, 1)
                act.wait_ge(n_pre, t + 1)
                nc.scalar.activation(act_out[:, 4:6], npre, ACT.Tanh).then_inc(n_s, 1)

            steps(act, time_step)

        @block.vector
        def _(dve):
            for s in (r_pre, n_sum, z_pre):
                dve.sem_inc(s, 1)
            nc.vector.tensor_copy(bn, m.bhh_n.unsqueeze(2).broadcast_to([P, KT, B])).then_inc(bn_s, 1)
            c = Chain(dve, step)
            c.link(nc.vector.tensor_copy(h[:, 0], m.condT[:]))
            c.link(nc.vector.tensor_copy(hparts(0, 0), h[:, 0]))
            c.link(nc.vector.tensor_tensor(rest, h[:, 0], hparts(0, 0), ALU.subtract))
            c.link(nc.vector.tensor_copy(hparts(0, 1), rest))
            nc.vector.tensor_tensor(hparts(0, 2), rest, hparts(0, 1), ALU.subtract).then_inc(h_s, 1)
            base = c.n

            def time_step(t, u):
                v = nc.vector
                c = Chain(dve, step, LINKS * t + base)
                dve.wait_ge(r_ps, t + 1)
                v.tensor_reduce(pre[:, 0:2], parts_sum(RB), AX.X, ALU.add).then_inc(r_pre, 1)
                dve.wait_ge(n_ps, t + 1)
                v.tensor_reduce(pre[:, 4:6], parts_sum(NB), AX.X, ALU.add).then_inc(n_sum, 1)
                dve.wait_ge(n_sum, t + 2)
                dve.wait_ge(r_s, t + 1)
                v.tensor_tensor(rn, pre[:, 4:6], act_out[:, 0:2], ALU.mult).then_inc(step, 1)
                dve.wait_ge(z_ps, t + 1)
                v.tensor_reduce(pre[:, 2:4], parts_sum(ZB), AX.X, ALU.add).then_inc(z_pre, 1)
                dve.wait_ge(step, LINKS * t + base + 1)
                v.tensor_tensor(npre, rn, gi[:, bass.ds(t, 1), 4 * B:6 * B].rearrange("p o (c b) -> p (o c) b", b=B),
                                ALU.add).then_inc(n_pre, 1)
                dve.wait_ge(z_s, t + 1)
                v.tensor_tensor(zh, act_out[:, 2:4], h[:, u], ALU.mult).then_inc(step, 1)
                dve.wait_ge(n_s, t + 1)
                v.scalar_tensor_tensor(out=mn, in0=act_out[:, 2:4], scalar=1.0, in1=act_out[:, 4:6],
                                       op0=ALU.subtract, op1=ALU.mult).then_inc(step, 1)
                dve.wait_ge(kept, t + 1)
                dve.wait_ge(step, LINKS * t + base + 3)
                v.tensor_tensor(hparts(1 - u, 0), zh, mn, ALU.subtract)
                v.tensor_tensor(h[:, 1 - u], zh, mn, ALU.subtract).then_inc(state_s, 1)
                dve.wait_ge(state_s, t + 1)
                v.tensor_tensor(rest, h[:, 1 - u], hparts(1 - u, 0), ALU.subtract)
                v.tensor_tensor(hparts(1 - u, 1), h[:, 1 - u], hparts(1 - u, 0), ALU.subtract).then_inc(rest_s, 1)
                dve.wait_ge(rest_s, t + 1)
                v.tensor_tensor(hparts(1 - u, 2), rest, hparts(1 - u, 1), ALU.subtract).then_inc(h_s, 1)

            steps(dve, time_step)
            for q in range(B // 2):
                dve.wait_ge(turned, q + 1)
                if q >= 2:
                    dve.wait_ge(stored[q % 2], 16 * (q // 2))
                nc.vector.tensor_tensor(res[:, q % 2], m.ps[:, 4 + q % 4], m.X[:, 2 * q:2 * q + 2].rearrange("p b d -> p (b d)"),
                                        ALU.add).then_inc(summed, 1)

        @block.gpsimd
        def _(pool):
            pool.sem_inc(kept, 2)

            def time_step(t, u):
                pool.wait_ge(state_s, t + 1)
                carry(pool, m)
                nc.gpsimd.tensor_copy(hist[:, :, :, bass.ds(t, 1)].rearrange("p k b o -> p k (b o)"), h[:, 1 - u]).then_inc(kept, 1)

            steps(pool, time_step)

        @block.sync
        def _(sp):
            for q in range(B // 2):
                sp.wait_ge(summed, q + 1)
                sp.dma_start(out[2 * q:2 * q + 2].rearrange("b t d -> t b d"), res[:, q % 2].rearrange("p (b d) -> p b d", b=2)
                             ).then_inc(stored[q % 2], 16)
            for u in range(2):
                sp.wait_ge(stored[u], 16 * (B // 4))


def kernel(**inputs):
    import numpy as np
    import concourse.bacc as bacc
    from concourse.bass_utils import run_bass_kernel_spmd

    laid = {n: np.ascontiguousarray(v) for n, v in inputs.items()}
    laid["condT"] = np.ascontiguousarray(laid["cond_2048"].T)
    for g in "qkv":
        laid[f"W{g}T"] = np.ascontiguousarray(laid.pop(f"L0_cond_W{g}").T)
    for g in "qk":
        laid[f"W{g}T"] = np.ascontiguousarray(laid[f"W{g}T"].reshape(P, H, DH0).transpose(0, 2, 1).reshape(P, P))
    for n in ("L1_cond_b_emb", "L2_cond_ada_b", "L1_cond_g_norm", "L2_cond_qkv_b", "L2_cond_out_b", "L2_cond_ffn_b1",
              "L2_cond_ffn_b2", "L3_cond_b_ih", "L3_cond_b_hh"):
        laid["col_" + n] = np.ascontiguousarray(laid.pop(n).reshape(-1, P).T)
    nc = bacc.Bacc("TRN2", target_bir_lowering=False, num_devices=1)
    args = {n: nc.dram_tensor(f"in_{n}", v.shape, mybir.dt.from_np(v.dtype), kind="ExternalInput").ap()
            for n, v in laid.items()}
    out = nc.dram_tensor("out", (B, N, D), F32, kind="ExternalOutput").ap()
    program(nc, args, out)
    r = run_bass_kernel_spmd(nc, [{f"in_{n}": v for n, v in laid.items()}], core_ids=[0])
    return r.results[0]["out"]
```
